# Optimizing a Trainium2 kernel written in Bass

```python
import numpy as np
import jax
import jax.numpy as jnp

def _softmax(x, axis=-1):
    return jax.nn.softmax(x, axis=axis)

def _gelu(x):
    return jax.nn.gelu(x, approximate=True)

def _silu(x):
    return jax.nn.silu(x)

def _sigmoid(x):
    return jax.nn.sigmoid(x)

def _layernorm(x, axis=-1, eps=1e-05):
    m = jnp.mean(x, axis=axis, keepdims=True)
    v = jnp.var(x, axis=axis, keepdims=True)
    return (x - m) / jnp.sqrt(v + eps)

def _scatter_add(tgt, idx, src, axis=0):
    return tgt.at[idx].add(src)

def _segment_sum(src, seg, n):
    return jax.ops.segment_sum(src, seg, n)
kernel_name = 'mk_macaron_d2_jaxref_r4_aa718d'

def setup_inputs(seed: int=0):
    np.random.seed(seed)
    _w = jnp.asarray

    def _L0_attn_setup():
        import jax, jax.numpy as jnp
        import numpy as np
        N_HEAD = 16
        EPS = 1e-06

        def _linear_attention(q, k, v):
            B, H, D = (q.shape[1], q.shape[2], q.shape[3])

            def step(carry, qkv_t):
                S, z = carry
                qt, kt, vt = qkv_t
                S = S + kt[..., :, None] * vt[..., None, :]
                z = z + kt
                num = jnp.einsum('bhi,bhij->bhj', qt, S)
                den = jnp.sum(qt * z, axis=-1, keepdims=True)
                return ((S, z), num / (den + EPS))
            S0 = jnp.zeros((B, H, D, D), q.dtype)
            z0 = jnp.zeros((B, H, D), q.dtype)
            _, y = jax.lax.scan(step, (S0, z0), (q, k, v))
            return y
        key = jax.random.key(seed)
        k1, k2, k3 = jax.random.split(key, 3)
        B, T, C = (2, 512, 256)
        x = jax.random.normal(k1, (B, T, C), dtype=jnp.float32)
        w_attn = jax.random.normal(k2, (C, 3 * C), dtype=jnp.float32) * 0.02
        w_proj = jax.random.normal(k3, (C, C), dtype=jnp.float32) * 0.02
        return {'x': x, 'w_attn': w_attn, 'w_proj': w_proj}
    _L0_attn_in = _L0_attn_setup()

    def _L0_ffn_setup():
        import jax, jax.numpy as jnp
        import numpy as np
        DIM = 256
        DEPTH = 2
        HEADS = 8
        DIM_HEAD = 64
        WINDOW = 128
        INNER = HEADS * DIM_HEAD
        HID = int(DIM * 4 * 2 / 3)
        B, N = (2, 2048)
        QK_SCALE = 8.0

        def shift_token(t):
            t1, t2 = jnp.split(t, 2, axis=-1)
            t2 = jnp.pad(t2, ((0, 0), (1, 0), (0, 0)))[:, :-1]
            return jnp.concatenate([t1, t2], axis=-1)

        def l2norm(t):
            return t / jnp.clip(jnp.linalg.norm(t, axis=-1, keepdims=True), 1e-12)

        def rotate_half(x):
            x1, x2 = jnp.split(x, 2, axis=-1)
            return jnp.concatenate([-x2, x1], axis=-1)

        def rotary_xpos(q, k):
            n = q.shape[-2]
            half_idx = jnp.arange(0, DIM_HEAD, 2, dtype=jnp.float32)
            inv_freq = 1.0 / 10000.0 ** (half_idx / DIM_HEAD)
            t = jnp.arange(n, dtype=jnp.float32)
            freqs = t[:, None] * inv_freq[None, :]
            freqs = jnp.concatenate([freqs, freqs], axis=-1)
            base = (half_idx + 0.4 * DIM_HEAD) / (1.4 * DIM_HEAD)
            power = (t - n // 2) / float(WINDOW // 2)
            scale = base[None, :] ** power[:, None]
            scale = jnp.concatenate([scale, scale], axis=-1)
            cos, sin = (jnp.cos(freqs), jnp.sin(freqs))
            q = q * cos * scale + rotate_half(q) * sin * scale
            k = k * cos / scale + rotate_half(k) * sin / scale
            return (q, k)

        def local_attention(q, k, v):
            b, h, n, d = q.shape
            w = n // WINDOW
            bq = q.reshape(b, h, w, WINDOW, d) * QK_SCALE
            bk = k.reshape(b, h, w, WINDOW, d)
            bv = v.reshape(b, h, w, WINDOW, d)

            def look_around(t):
                p = jnp.pad(t, ((0, 0), (0, 0), (1, 0), (0, 0), (0, 0)))
                return jnp.concatenate([p[:, :, :w], p[:, :, 1:]], axis=3)
            bk, bv = (look_around(bk), look_around(bv))
            bt = jnp.arange(n).reshape(w, WINDOW)
            btp = jnp.pad(bt, ((1, 0), (0, 0)), constant_values=-1)
            btk = jnp.concatenate([btp[:w], btp[1:]], axis=1)
            sim = jnp.einsum('bhwid,bhwjd->bhwij', bq, bk)
            i = bt[:, :, None]
            j = btk[:, None, :]
            mask = (i < j) | (i > j + WINDOW) | (j == -1)
            sim = jnp.where(mask, -jnp.finfo(sim.dtype).max, sim)
            attn = jax.nn.softmax(sim, axis=-1)
            out = jnp.einsum('bhwij,bhwjd->bhwid', attn, bv)
            return out.reshape(b, h, n, d)

        def _layer(x, wqkv, qs, ksc, wo, lg, lb, w1, b1, w2, b2):
            b, n, _ = x.shape
            h = shift_token(x)
            qkv = h @ wqkv
            q, k, v = jnp.split(qkv, 3, axis=-1)
            to_heads = lambda t: t.reshape(b, n, HEADS, DIM_HEAD).transpose(0, 2, 1, 3)
            q, k, v = (to_heads(q), to_heads(k), to_heads(v))
            q = l2norm(q) * qs
            k = l2norm(k) * ksc
            q, k = rotary_xpos(q, k)
            o = local_attention(q, k, v)
            o = o.transpose(0, 2, 1, 3).reshape(b, n, INNER)
            x = x + o @ wo
            h = shift_token(x)
            mu = h.mean(-1, keepdims=True)
            var = h.var(-1, keepdims=True)
            h = (h - mu) / jnp.sqrt(var + 1e-05) * lg + lb
            h = h @ w1 + b1
            a, g = jnp.split(h, 2, axis=-1)
            h = a * jax.nn.gelu(g, approximate=False)
            x = x + h @ w2 + b2
            return x
        key = jax.random.key(seed)
        ks = jax.random.split(key, 6)
        return {'x': jax.random.normal(ks[0], (B, N, DIM), jnp.float32), 'wqkv': jax.random.normal(ks[1], (DEPTH, DIM, 3 * INNER), jnp.float32) * 0.02, 'q_scale': jnp.ones((DEPTH, DIM_HEAD), jnp.float32), 'k_scale': jnp.ones((DEPTH, DIM_HEAD), jnp.float32), 'wo': jax.random.normal(ks[2], (DEPTH, INNER, DIM), jnp.float32) * 0.02, 'ln_g': jnp.ones((DEPTH, DIM), jnp.float32), 'ln_b': jnp.zeros((DEPTH, DIM), jnp.float32), 'w1': jax.random.normal(ks[3], (DEPTH, DIM, 2 * HID), jnp.float32) * 0.02, 'b1': jnp.zeros((DEPTH, 2 * HID), jnp.float32), 'w2': jax.random.normal(ks[4], (DEPTH, HID, DIM), jnp.float32) * 0.02, 'b2': jnp.zeros((DEPTH, DIM), jnp.float32)}
    _L0_ffn_in = _L0_ffn_setup()

    def _L1_attn_setup():
        import jax, jax.numpy as jnp
        import numpy as np
        B, N, D, H = (4, 2048, 256, 16)
        HD = D // H
        EPS = 1e-05

        def _abs_clamp(t, min_mag=0.01, max_mag=100.0):
            return jnp.clip(jnp.abs(t), min_mag, max_mag) * jnp.sign(t)

        def _heads(x):
            b, n, _ = x.shape
            return x.reshape(b, n, H, HD).transpose(0, 2, 1, 3)
        key = jax.random.key(seed)
        ks = jax.random.split(key, 12)
        s = 1.0 / np.sqrt(D)
        return {'query': jax.random.normal(ks[0], (B, N, D), jnp.float32), 'Wq': jax.random.normal(ks[1], (D, D), jnp.float32) * s, 'bq': jax.random.normal(ks[2], (D,), jnp.float32) * 0.01, 'Wk': jax.random.normal(ks[3], (D, D), jnp.float32) * s, 'bk': jax.random.normal(ks[4], (D,), jnp.float32) * 0.01, 'Wv': jax.random.normal(ks[5], (D, D), jnp.float32) * s, 'bv': jax.random.normal(ks[6], (D,), jnp.float32) * 0.01, 'Wu': jax.random.normal(ks[7], (D, D), jnp.float32) * s, 'bu': jax.random.normal(ks[8], (D,), jnp.float32) * 0.01, 'Wo': jax.random.normal(ks[9], (D, D), jnp.float32) * s, 'bo': jax.random.normal(ks[10], (D,), jnp.float32) * 0.01, 'ln_w': jnp.ones((D,), jnp.float32), 'ln_b': jnp.zeros((D,), jnp.float32)}
    _L1_attn_in = _L1_attn_setup()

    def _L1_ffn_setup():
        import jax, jax.numpy as jnp
        import numpy as np
        EPS = 1e-05

        def _quantize(W):
            gamma = jnp.mean(jnp.abs(W))
            return jnp.clip(jnp.round(W / (gamma + EPS)), -1.0, 1.0)
        key = jax.random.key(seed)
        k_x, k_w1, k_b1, k_w2, k_b2 = jax.random.split(key, 5)
        n_embd = 256
        d_ff = 4 * n_embd
        B, S = (4, 1024)
        bound1 = 1.0 / np.sqrt(n_embd)
        bound2 = 1.0 / np.sqrt(d_ff)
        x = jax.random.normal(k_x, (B, S, n_embd), dtype=jnp.float32)
        W1 = jax.random.uniform(k_w1, (d_ff, n_embd), jnp.float32, -bound1, bound1)
        b1 = jax.random.uniform(k_b1, (d_ff,), jnp.float32, -bound1, bound1)
        W2 = jax.random.uniform(k_w2, (n_embd, d_ff), jnp.float32, -bound2, bound2)
        b2 = jax.random.uniform(k_b2, (n_embd,), jnp.float32, -bound2, bound2)
        return {'x': x, 'W1': W1, 'b1': b1, 'W2': W2, 'b2': b2}
    _L1_ffn_in = _L1_ffn_setup()
    _d = {'L0_attn_x': _L0_attn_in['x'], 'L0_attn_w_attn': _L0_attn_in['w_attn'], 'L0_attn_w_proj': _L0_attn_in['w_proj'], 'L0_ffn_wqkv': _L0_ffn_in['wqkv'], 'L0_ffn_q_scale': _L0_ffn_in['q_scale'], 'L0_ffn_k_scale': _L0_ffn_in['k_scale'], 'L0_ffn_wo': _L0_ffn_in['wo'], 'L0_ffn_ln_g': _L0_ffn_in['ln_g'], 'L0_ffn_ln_b': _L0_ffn_in['ln_b'], 'L0_ffn_w1': _L0_ffn_in['w1'], 'L0_ffn_b1': _L0_ffn_in['b1'], 'L0_ffn_w2': _L0_ffn_in['w2'], 'L0_ffn_b2': _L0_ffn_in['b2'], 'L1_attn_Wq': _L1_attn_in['Wq'], 'L1_attn_bq': _L1_attn_in['bq'], 'L1_attn_Wk': _L1_attn_in['Wk'], 'L1_attn_bk': _L1_attn_in['bk'], 'L1_attn_Wv': _L1_attn_in['Wv'], 'L1_attn_bv': _L1_attn_in['bv'], 'L1_attn_Wu': _L1_attn_in['Wu'], 'L1_attn_bu': _L1_attn_in['bu'], 'L1_attn_Wo': _L1_attn_in['Wo'], 'L1_attn_bo': _L1_attn_in['bo'], 'L1_attn_ln_w': _L1_attn_in['ln_w'], 'L1_attn_ln_b': _L1_attn_in['ln_b'], 'L1_ffn_W1': _L1_ffn_in['W1'], 'L1_ffn_b1': _L1_ffn_in['b1'], 'L1_ffn_W2': _L1_ffn_in['W2'], 'L1_ffn_b2': _L1_ffn_in['b2']}
    _x0 = _d['L0_attn_x']
    _d['L0_attn_x'] = jax.random.normal(jax.random.fold_in(jax.random.key(seed), 1), (4, 1024, 256), dtype=_x0.dtype)
    del _x0
    return _d

def reference(L0_attn_x, L0_attn_w_attn, L0_attn_w_proj, L0_ffn_wqkv, L0_ffn_q_scale, L0_ffn_k_scale, L0_ffn_wo, L0_ffn_ln_g, L0_ffn_ln_b, L0_ffn_w1, L0_ffn_b1, L0_ffn_w2, L0_ffn_b2, L1_attn_Wq, L1_attn_bq, L1_attn_Wk, L1_attn_bk, L1_attn_Wv, L1_attn_bv, L1_attn_Wu, L1_attn_bu, L1_attn_Wo, L1_attn_bo, L1_attn_ln_w, L1_attn_ln_b, L1_ffn_W1, L1_ffn_b1, L1_ffn_W2, L1_ffn_b2):

    def _L0_attn_ref(x, w_attn, w_proj):
        import jax, jax.numpy as jnp
        import numpy as np
        N_HEAD = 16
        EPS = 1e-06

        def _linear_attention(q, k, v):
            B, H, D = (q.shape[1], q.shape[2], q.shape[3])

            def step(carry, qkv_t):
                S, z = carry
                qt, kt, vt = qkv_t
                S = S + kt[..., :, None] * vt[..., None, :]
                z = z + kt
                num = jnp.einsum('bhi,bhij->bhj', qt, S)
                den = jnp.sum(qt * z, axis=-1, keepdims=True)
                return ((S, z), num / (den + EPS))
            S0 = jnp.zeros((B, H, D, D), q.dtype)
            z0 = jnp.zeros((B, H, D), q.dtype)
            _, y = jax.lax.scan(step, (S0, z0), (q, k, v))
            return y
        B, T, C = x.shape
        H = N_HEAD
        D = C // H
        qkv = x @ w_attn
        q, k, v = jnp.split(qkv, 3, axis=-1)

        def to_tbhd(a):
            return a.reshape(B, T, H, D).transpose(1, 0, 2, 3)
        q = jax.nn.elu(to_tbhd(q)) + 1.0
        k = jax.nn.elu(to_tbhd(k)) + 1.0
        v = to_tbhd(v)
        y = _linear_attention(q, k, v)
        y = y.transpose(1, 0, 2, 3).reshape(B, T, C)
        return y @ w_proj

    def _L0_ffn_ref(x, wqkv, q_scale, k_scale, wo, ln_g, ln_b, w1, b1, w2, b2):
        import jax, jax.numpy as jnp
        import numpy as np
        DIM = 256
        DEPTH = 2
        HEADS = 8
        DIM_HEAD = 64
        WINDOW = 128
        INNER = HEADS * DIM_HEAD
        HID = int(DIM * 4 * 2 / 3)
        B, N = (2, 2048)
        QK_SCALE = 8.0

        def shift_token(t):
            t1, t2 = jnp.split(t, 2, axis=-1)
            t2 = jnp.pad(t2, ((0, 0), (1, 0), (0, 0)))[:, :-1]
            return jnp.concatenate([t1, t2], axis=-1)

        def l2norm(t):
            return t / jnp.clip(jnp.linalg.norm(t, axis=-1, keepdims=True), 1e-12)

        def rotate_half(x):
            x1, x2 = jnp.split(x, 2, axis=-1)
            return jnp.concatenate([-x2, x1], axis=-1)

        def rotary_xpos(q, k):
            n = q.shape[-2]
            half_idx = jnp.arange(0, DIM_HEAD, 2, dtype=jnp.float32)
            inv_freq = 1.0 / 10000.0 ** (half_idx / DIM_HEAD)
            t = jnp.arange(n, dtype=jnp.float32)
            freqs = t[:, None] * inv_freq[None, :]
            freqs = jnp.concatenate([freqs, freqs], axis=-1)
            base = (half_idx + 0.4 * DIM_HEAD) / (1.4 * DIM_HEAD)
            power = (t - n // 2) / float(WINDOW // 2)
            scale = base[None, :] ** power[:, None]
            scale = jnp.concatenate([scale, scale], axis=-1)
            cos, sin = (jnp.cos(freqs), jnp.sin(freqs))
            q = q * cos * scale + rotate_half(q) * sin * scale
            k = k * cos / scale + rotate_half(k) * sin / scale
            return (q, k)

        def local_attention(q, k, v):
            b, h, n, d = q.shape
            w = n // WINDOW
            bq = q.reshape(b, h, w, WINDOW, d) * QK_SCALE
            bk = k.reshape(b, h, w, WINDOW, d)
            bv = v.reshape(b, h, w, WINDOW, d)

            def look_around(t):
                p = jnp.pad(t, ((0, 0), (0, 0), (1, 0), (0, 0), (0, 0)))
                return jnp.concatenate([p[:, :, :w], p[:, :, 1:]], axis=3)
            bk, bv = (look_around(bk), look_around(bv))
            bt = jnp.arange(n).reshape(w, WINDOW)
            btp = jnp.pad(bt, ((1, 0), (0, 0)), constant_values=-1)
            btk = jnp.concatenate([btp[:w], btp[1:]], axis=1)
            sim = jnp.einsum('bhwid,bhwjd->bhwij', bq, bk)
            i = bt[:, :, None]
            j = btk[:, None, :]
            mask = (i < j) | (i > j + WINDOW) | (j == -1)
            sim = jnp.where(mask, -jnp.finfo(sim.dtype).max, sim)
            attn = jax.nn.softmax(sim, axis=-1)
            out = jnp.einsum('bhwij,bhwjd->bhwid', attn, bv)
            return out.reshape(b, h, n, d)

        def _layer(x, wqkv, qs, ksc, wo, lg, lb, w1, b1, w2, b2):
            b, n, _ = x.shape
            h = shift_token(x)
            qkv = h @ wqkv
            q, k, v = jnp.split(qkv, 3, axis=-1)
            to_heads = lambda t: t.reshape(b, n, HEADS, DIM_HEAD).transpose(0, 2, 1, 3)
            q, k, v = (to_heads(q), to_heads(k), to_heads(v))
            q = l2norm(q) * qs
            k = l2norm(k) * ksc
            q, k = rotary_xpos(q, k)
            o = local_attention(q, k, v)
            o = o.transpose(0, 2, 1, 3).reshape(b, n, INNER)
            x = x + o @ wo
            h = shift_token(x)
            mu = h.mean(-1, keepdims=True)
            var = h.var(-1, keepdims=True)
            h = (h - mu) / jnp.sqrt(var + 1e-05) * lg + lb
            h = h @ w1 + b1
            a, g = jnp.split(h, 2, axis=-1)
            h = a * jax.nn.gelu(g, approximate=False)
            x = x + h @ w2 + b2
            return x
        for l in range(DEPTH):
            x = _layer(x, wqkv[l], q_scale[l], k_scale[l], wo[l], ln_g[l], ln_b[l], w1[l], b1[l], w2[l], b2[l])
        return x

    def _L1_attn_ref(query, Wq, bq, Wk, bk, Wv, bv, Wu, bu, Wo, bo, ln_w, ln_b):
        import jax, jax.numpy as jnp
        import numpy as np
        B, N, D, H = (4, 2048, 256, 16)
        HD = D // H
        EPS = 1e-05

        def _abs_clamp(t, min_mag=0.01, max_mag=100.0):
            return jnp.clip(jnp.abs(t), min_mag, max_mag) * jnp.sign(t)

        def _heads(x):
            b, n, _ = x.shape
            return x.reshape(b, n, H, HD).transpose(0, 2, 1, 3)
        q = jax.nn.relu(_heads(query @ Wq + bq))
        k = jax.nn.relu(_heads(query @ Wk + bk))
        v = _heads(query @ Wv + bv)
        u = query @ Wu + bu
        kv = jnp.einsum('bhnd,bhne->bhde', k, v)
        kv = _abs_clamp(kv)
        out = jnp.einsum('bhnd,bhde->bhne', q, kv)
        out = out.transpose(0, 2, 1, 3).reshape(query.shape)
        mu = jnp.mean(out, axis=-1, keepdims=True)
        var = jnp.var(out, axis=-1, keepdims=True)
        out = (out - mu) * jax.lax.rsqrt(var + EPS) * ln_w + ln_b
        out = u * out
        return out @ Wo + bo

    def _L1_ffn_ref(x, W1, b1, W2, b2):
        import jax, jax.numpy as jnp
        import numpy as np
        EPS = 1e-05

        def _quantize(W):
            gamma = jnp.mean(jnp.abs(W))
            return jnp.clip(jnp.round(W / (gamma + EPS)), -1.0, 1.0)
        Wq1 = _quantize(W1)
        Wq2 = _quantize(W2)
        h = jax.nn.relu(jnp.einsum('bsd,fd->bsf', x, Wq1) + b1)
        out = jnp.einsum('bsf,df->bsd', h, Wq2) + b2
        return out
    x = L0_attn_x
    x = x + 0.5 * _L0_ffn_ref(_layernorm(x, axis=-1), L0_ffn_wqkv, L0_ffn_q_scale, L0_ffn_k_scale, L0_ffn_wo, L0_ffn_ln_g, L0_ffn_ln_b, L0_ffn_w1, L0_ffn_b1, L0_ffn_w2, L0_ffn_b2)
    x = x + _L0_attn_ref(_layernorm(x, axis=-1), L0_attn_w_attn, L0_attn_w_proj)
    x = x + 0.5 * _L0_ffn_ref(_layernorm(x, axis=-1), L0_ffn_wqkv, L0_ffn_q_scale, L0_ffn_k_scale, L0_ffn_wo, L0_ffn_ln_g, L0_ffn_ln_b, L0_ffn_w1, L0_ffn_b1, L0_ffn_w2, L0_ffn_b2)
    x = x + 0.5 * _L1_ffn_ref(_layernorm(x, axis=-1), L1_ffn_W1, L1_ffn_b1, L1_ffn_W2, L1_ffn_b2)
    x = x + _L1_attn_ref(_layernorm(x, axis=-1), L1_attn_Wq, L1_attn_bq, L1_attn_Wk, L1_attn_bk, L1_attn_Wv, L1_attn_bv, L1_attn_Wu, L1_attn_bu, L1_attn_Wo, L1_attn_bo, L1_attn_ln_w, L1_attn_ln_b)
    x = x + 0.5 * _L1_ffn_ref(_layernorm(x, axis=-1), L1_ffn_W1, L1_ffn_b1, L1_ffn_W2, L1_ffn_b2)
    return x

_drawn_inputs = setup_inputs


def setup_inputs(seed=0):
    import zlib

    import numpy as np

    out = dict(_drawn_inputs(seed))
    spreads = {'L0_ffn_q_scale': (1.0, 0.6),
     'L0_ffn_k_scale': (1.0, 0.6),
     'L0_ffn_ln_g': (1.0, 0.6),
     'L0_ffn_ln_b': (0.0, 0.8),
     'L0_ffn_b1': (0.0, 0.8),
     'L0_ffn_b2': (0.0, 0.1),
     'L1_attn_ln_w': (1.0, 0.6),
     'L1_attn_ln_b': (0.0, 0.8)}
    factors = {'L0_attn_w_attn': 8.0,
     'L0_attn_w_proj': 8.0,
     'L0_ffn_wqkv': 3.5,
     'L0_ffn_wo': 3.499,
     'L1_attn_Wq': 8.0,
     'L1_attn_bq': 200.0,
     'L1_attn_Wk': 8.0,
     'L1_attn_bk': 200.0,
     'L1_attn_Wv': 8.0,
     'L1_attn_bv': 8.0,
     'L1_attn_Wu': 8.0,
     'L1_attn_bu': 64.0,
     'L1_attn_Wo': 8.0,
     'L1_attn_bo': 200.0,
     'L1_ffn_b1': 8.0,
     'L1_ffn_b2': 200.0}
    for name, (base, spread) in spreads.items():
        noise = np.random.default_rng([zlib.crc32(name.encode()), seed]).standard_normal(out[name].shape)
        drawn = base * np.exp(spread * noise) if base else spread * noise
        out[name] = jnp.asarray(drawn.astype(out[name].dtype))
    for name, factor in factors.items():
        out[name] = (out[name] * factor).astype(out[name].dtype)
    return out
```

```python
from contextlib import ExitStack

import numpy as np

import concourse.bass as bass
from concourse import mybir

F32 = mybir.dt.float32
F32R = mybir.dt.float32r
BF16 = mybir.dt.bfloat16
ALU = mybir.AluOpType
ACT = mybir.ActivationFunctionType
AX = mybir.AxisListType

P = 128
B, N, D = 4, 1024, 256
TB = N // P
NT = B * TB
KD = D // P
DEPTH = 2
NRUN = 2 * DEPTH
HEADS, DH = 8, 64
INNER = HEADS * DH
KI = INNER // P
HID = D * 4 * 2 // 3
CH = -(-HID // P)
HTAIL = HID - (CH - 1) * P
TAILG = 64
U = 4
NIT = NT // U
GRP = NIT
SCALE = 8.0
BIG = -3.0e38
H0, D0 = 16, 16
VA = D0 + 1
FF = 1024
CF = FF // P
OFF = 16

PAIRS = [(0, 2), (1, 3), (4, 6), (5, 7)]
NG = len(PAIRS)

ATTN = {
    "pe": """sc0+0 pt3-1 k+2 pv2-1 sc1+0 pv3-1 sc2+0 pt0+0 v+2 pt1+0 ot-1 ht+3 qT+1 sc3+0 pv0+0 wo-1 kT+1
             pv1+0 pt2+0 q+3""",
    "dv": """norm_k+1 wo-2 q+2 sum_q+2 rs-1 sc1+0 on-1 k+2 sc2+0 sum_k+2 ot-1 qT+1 sc3+0 ht+3 kT+1 norm_q+2
             sc0+1""",
    "ac": """sc3-1 kT+0 pt2-1 pt3-1 q+2 k+2 sc0+0 sc1+0 pt0+0 v+2 ot-1 qT+1 ht+3 sc2+0 pt1+0""",
    "pl": "add_q+1 add_k+1 sum_k+1",
    "sp": "wo-2 ld+4",
}


class Ev:

    def __init__(self, handle):
        self.h = handle

    def inc(self, ins, n=1):
        ins.then_inc(self.h, n)

    def wait(self, e, n):
        e.wait_ge(self.h, n + OFF)

    def wait_alone(self, e, n, passed):
        e.wait_ge(self.h, n + OFF)
        e.sem_inc(passed, 1)


def shape_constants():
    f = np.float32
    half = np.arange(0, DH, 2, dtype=f)
    inv = (f(1.0) / np.power(f(10000.0), half / f(DH))).astype(f)
    t = np.arange(N, dtype=f)
    fr = t[:, None] * inv[None, :]
    fr = np.concatenate([fr, fr], -1)
    base = (half + f(0.4 * DH)) / f(1.4 * DH)
    power = (t - f(N // 2)) / f(64.0)
    sc = np.power(base[None, :], power[:, None]).astype(f)
    sc = np.concatenate([sc, sc], -1)
    sign = np.concatenate([-np.ones(DH // 2, f), np.ones(DH // 2, f)])
    cos, sin = np.cos(fr).astype(f), np.sin(fr).astype(f)
    tabs = [SCALE * cos * sc, SCALE * sin * sc * sign, cos / sc, sin / sc * sign]
    rot = np.stack([a.astype(f).reshape(TB, P, DH).transpose(1, 0, 2) for a in tabs], 1)
    q, k = np.arange(P)[:, None], np.arange(P)[None, :]
    cur = np.where(k <= q, 0, BIG).astype(f)
    prv = np.where(k >= q, 0, BIG).astype(f)
    off = np.full((P, P), BIG, f)
    sel = np.stack([off if i % 2 == 0 else prv for i in range(NIT)], 1)
    masks = np.concatenate([cur, prv, cur, prv, prv, cur, prv, cur, sel.reshape(P, -1)], 1)
    causal = (q <= k).astype(f)
    keep = np.ones((P, NT), f)
    keep[:, TB - 1::TB] = 0
    bd = np.zeros((P, 4, VA), f)
    for r in range(4):
        bd[32 * r:32 * r + D0, r] = 1
    bd1 = np.kron(np.eye(P // D0, dtype=f), np.ones((D0, D0), f))
    misc = np.concatenate([np.eye(P, dtype=f), causal, bd.reshape(P, -1), bd1, keep], 1)
    return {"c_rot": np.ascontiguousarray(rot.reshape(P, -1)), "c_mask": masks, "c_misc": misc}


MI, MC, MB, MD, MK = 0, P, 2 * P, 2 * P + 4 * VA, 3 * P + 4 * VA
MISC = MK + NT


def build(nc, a, out):
    ctx = ExitStack()
    with ctx:
        scope = [ctx]

        def sb(name, shape, dt=F32):
            return scope[-1].enter_context(nc.sbuf_tensor(name, shape, dt))

        def ev(name):
            return Ev(ctx.enter_context(nc.semaphore(name)))

        ya = nc.dram_tensor("ya", (B * (N + 1), P), F32, kind="Internal").ap()
        yb = nc.dram_tensor("yb", (B * (N + 1), P), F32, kind="Internal").ap()
        x_v = a["L0_attn_x"].rearrange("b (t p) c -> p (b t) c", p=P)
        out_v = out.rearrange("b (t p) c -> p (b t) c", p=P)

        bank = [ctx.enter_context(nc.psum_tensor(f"bank{i}", [P, 512], F32)) for i in range(8)]

        X = sb("X", [P, NT, D])
        Y = sb("Y", [P, NT, D])
        raw = sb("raw", [P, 3072])
        raw2 = sb("raw2", [P, 2048])
        misc = sb("misc", [P, MISC])
        identf = misc[:, MI:MI + P]
        maskf = raw[:, 0:(4 + 4 + NIT) * P]
        maskb = sb("maskb", [P, (4 + 4 + NIT) * P], BF16)
        maskE, maskO = maskb[:, 0:512], maskb[:, 512:1024]
        masksel = maskb[:, 1024:].rearrange("p (i k) -> p i k", i=NIT)
        mask0 = sb("mask0", [P, 512], BF16)
        identb = sb("identb", [P, P], BF16)
        ones = sb("ones", [P, P])
        mhalf = sb("mhalf", [P, 16])
        eps = sb("eps", [P, TB])
        zrow = sb("zrow", [B, P])
        rotc = sb("rotc", [P, 4, TB, DH])
        scales = sb("scales", [P, 2 * DH])
        brow = sb("brow", [P, D])
        vec = sb("vec", [P, 32])
        bias1 = sb("bias1", [P, 2 * CH + 4])

        s_init = ev("init")
        s_raw, s_raw2, s_small = ev("raw"), ev("raw2"), ev("small")
        s_prepA, s_prepB, s_prepV, s_prepP = ev("prepA"), ev("prepB"), ev("prepV"), ev("prepP")

        scope.append(ExitStack())
        wq_h, wq_l = sb("wqkv_hi", [P, KD, 3 * INNER], F32R), sb("wqkv_lo", [P, KD, 3 * INNER], F32R)
        wo_h, wo_l = sb("wo_hi", [P, KI, D], F32R), sb("wo_lo", [P, KI, D], F32R)
        rot = sb("rot", [P, 4, TB, DH])
        H = [sb(f"H{i}", [P, D]) for i in range(U)]
        hTh = [sb(f"hT_hi{i}", [P, D], F32R) for i in range(2)]
        hTl = [sb(f"hT_lo{i}", [P, D], F32R) for i in range(2)]
        t1 = sb("rot_t1", [P, 2 * INNER])
        t2 = sb("rot_t2", [P, 2 * INNER])
        qk = [sb(f"qk{i}", [P, 2 * INNER]) for i in range(2)]
        ss, rn = sb("ss", [P, 16]), sb("rn", [P, 16])
        qTh = [sb(f"qT_hi{i}", [P, INNER], F32R) for i in range(2)]
        qTl = [sb(f"qT_lo{i}", [P, INNER], F32R) for i in range(2)]
        kTh, kTl = sb("kT_hi", [P, KI, 2, P], F32R), sb("kT_lo", [P, KI, 2, P], F32R)
        V = [sb(f"V{i}", [P, INNER]) for i in range(U)]
        nm = [sb(f"nmax{i}", [P, HEADS]) for i in range(2)]
        sums = [sb(f"sums{i}", [P, HEADS]) for i in range(2)]
        Pb = [sb(f"prob{i}", [P, 512]) for i in range(2)]
        PTs = [sb(f"probT{i}", [P, 512]) for i in range(2)]
        rs = sb("rsum", [P, HEADS])
        On = sb("On", [P, INNER])
        OTh, OTl = sb("OT_hi", [P, INNER], F32R), sb("OT_lo", [P, INNER], F32R)
        scope.pop().close()

        scope.append(ExitStack())
        w1_h, w1_l = sb("w1_hi", [P, KD, (2 * CH - 1) * P], F32R), sb("w1_lo", [P, KD, (2 * CH - 1) * P], F32R)
        w2_h, w2_l = sb("w2_hi", [P, CF, D], F32R), sb("w2_lo", [P, CF, D], F32R)
        HB = sb("HB", [P, U, D])
        Xn = sb("Xn", [P, U, D])
        gTh, gTl = sb("gT_hi", [P, KD, 512], F32R), sb("gT_lo", [P, KD, 512], F32R)
        gate = [sb(f"gate{i}", [P, 512]) for i in range(2)]
        hid = [sb(f"hid{i}", [P, 512]) for i in range(2)]
        hidh, hidl = sb("hid_hi", [P, CF, 512], F32R), sb("hid_lo", [P, CF, 512], F32R)
        st = sb("stats", [P, U, 6])
        mv = sb("meanvar", [P, U, 2])
        rv = sb("rstd", [P, U])
        thr = sb("thr", [P, 4])
        scope.pop().close()

        scope.append(ExitStack())
        wa = raw[:, 0:KD * 3 * D].rearrange("p (k n) -> p k n", k=KD)
        wp = raw[:, KD * 3 * D:KD * 4 * D].rearrange("p (k n) -> p k n", k=KD)
        Xn0 = [sb(f"lnx{i}", [P, D]) for i in range(2)]
        st0, mv0, rv0 = sb("st0", [P, 2, 6]), sb("mv0", [P, 2, 2]), sb("rv0", [P, 2])
        h0 = [sb(f"h0T{i}", [P, D]) for i in range(2)]
        mn, ex = sb("qk_min", [P, 512]), sb("qk_exp", [P, 512])
        qkp = [sb(f"qk_pad{i}", [P, 2, H0, 32]) for i in range(2)]
        va = [sb(f"v_one{i}", [P, H0, VA]) for i in range(2)]
        qT0, kT0 = sb("linqT", [P, 4, P]), sb("linkT", [P, 4, P])
        at = [sb(f"at{i}", [P, 4, P]) for i in range(4)]
        Sbd = sb("state", [P, 4, 4 * VA])
        dl = sb("delta", [P, 4, 4 * VA])
        rc = sb("rden", [P, H0])
        dn = sb("den", [P, H0])
        y0 = sb("y0", [P, D])
        yT0 = sb("yT0", [P, D])
        scope.pop().close()

        scope.append(ExitStack())
        sb("kept_ternary", [P, 2 * KD * (2 * CH - 1) * P + CF * D])
        wkv = raw[:, 0:KD * 2 * D].rearrange("p (k n) -> p k n", k=KD)
        wqg, wug, wog = (raw[:, KD * D * i:KD * D * (i + 1)].rearrange("p (k n) -> p k n", k=KD) for i in (2, 3, 4))
        bkv = raw2[:, 0:2 * D]
        burow, lnw, lnb, borow = (raw2[:, D * i:D * (i + 1)] for i in (2, 3, 4, 5))
        Xn1 = [sb(f"lny{i}", [P, D]) for i in range(2)]
        st1, mv1, rv1 = sb("st1", [P, TB, 6]), sb("mv1", [P, TB, 2]), sb("rv1", [P, TB])
        st2, mv2, rv2 = sb("st2", [P, TB, 6]), sb("mv2", [P, TB, 2]), sb("rv2", [P, TB])
        h1 = sb("h1T", [P, KD, TB * P])
        kvb = [sb(f"kv{i}", [P, 2 * D]) for i in range(2)]
        kb = [sb(f"krelu{i}", [P, D]) for i in range(2)]
        ab, sg, ng = sb("kv_abs", [P, D]), sb("kv_sign", [P, D]), sb("kv_neg", [P, D])
        kvm = sb("kvm", [P, D])
        q1 = sb("q1T", [P, KD, TB * P])
        oA = sb("oA", [P, TB, D])
        us = [sb(f"u{i}", [P, D]) for i in range(2)]
        o1 = [sb(f"o1_{i}", [P, D]) for i in range(2)]
        y1 = [sb(f"y1_{i}", [P, D]) for i in range(2)]
        yT1 = [sb(f"y1T{i}", [P, D]) for i in range(2)]
        scope.pop().close()

        names = """peHT acHT dvHT peQK acSQ dvRT dvSS plAD plRN dvQN peKT acKT dvKT peV acV peS dvMX acEX pePT acPT pePV
        dvRS dvON peOT acOT dvOT peWO dvY plM0
        dvST dvAG plRV dvXN peTR acHI dvLO peG peA acU dvHD xxHH dvHL peW2 dvYB plB2 sHB
        mdvY""".split()
        s = {n: ev("s_" + n) for n in names}
        s_ld = [ev(f"s_ld{i}") for i in range(U)]
        s_st = [ev(f"s_st{i}") for i in range(U)]
        s_stb = ev("s_stb")
        s_x = ev("s_x")
        s_passed = ctx.enter_context(nc.semaphore("s_passed"))
        s_ln = {n: ev("s_ln" + n) for n in ("dvX", "dvST", "dvAG", "plRV", "dvXN", "sST")}
        z = {n: ev("z_" + n) for n in """dvST dvAG plRV dvXN peTR acHT peQK peV dvMN acEX dvQK acV peTQ acTQ
        peAT dvAT peNU peDL dvDL dvSB dvDN dvRC dvY peTY acTY pePR dvX""".split()}
        g = {n: ev("g_" + n) for n in """dvST dvAG plRV dvXN peTR acHT peKV dvKV acK peKK dvC peQ acQ peO dvS2 dvA2 acO
        plR2 peU dvO plO dvU dvY peTY acTY pePR dvX plBO""".split()}
        everything = ([s_init, s_raw, s_raw2, s_small, s_prepA, s_prepB, s_prepV, s_prepP, s_stb, s_x]
                      + s_ld + s_st + list(s.values()) + list(s_ln.values()) + list(z.values()) + list(g.values()))
        everything = [x for x in everything if x is not s_init]

        block = ctx.enter_context(nc.Block())

        def program(E, e):
            pe, ac, dv, pl, sp = E == "pe", E == "ac", E == "dv", E == "pl", E == "sp"
            prep = {"raw": 0, "raw2": 0, "small": 0, "A": 0, "B": 0, "V": 0, "P": 0}

            def loop(n, body):
                with e.Fori(0, n) as i:
                    body(i)

            def flat(ap):
                return ap.rearrange("p a c -> p (a c)")

            def tile(buf, T):
                return flat(buf[:, bass.ds(T, 1), :])

            def three(o, lh, ll, rh, rl, start, stop):
                e.matmul(o, lh, rh, start=start, stop=False)
                e.matmul(o, lh, rl, start=False, stop=False)
                return e.matmul(o, ll, rh, start=False, stop=stop)

            def load(dst, src, which, columns=False):
                if sp:
                    {"raw": s_raw, "raw2": s_raw2, "small": s_small}[which].inc(
                        e.dma_start(dst, src, allow_slow_non_contiguous=columns), 16)
                prep[which] += 16

            def loaded(which):
                {"raw": s_raw, "raw2": s_raw2, "small": s_small}[which].wait(e, prep[which])

            def dve(f):
                if dv:
                    s_prepV.inc(f())
                prep["V"] += 1

            def act(f):
                if ac:
                    s_prepA.inc(f())
                prep["A"] += 1

            def pool(f):
                if pl:
                    s_prepB.inc(f())
                prep["B"] += 1

            def tens(f):
                if pe:
                    s_prepP.inc(f())
                prep["P"] += 1

            def sync(who, *on):
                if who == E:
                    for x in on:
                        {"V": s_prepV, "A": s_prepA, "B": s_prepB, "P": s_prepP}[x].wait(e, prep[x])

            if sp:
                for x in everything:
                    e.sem_inc(x.h, OFF)

            load(misc[:, :], a["c_misc"], "small")
            load(maskf, a["c_mask"], "raw")
            load(rotc[:, :, :, :].rearrange("p a t d -> p (a t d)"), a["c_rot"], "small")
            if not sp:
                loaded("small")
                loaded("raw")
            dve(lambda: e.tensor_copy(maskb[:, :], maskf))
            dve(lambda: e.tensor_copy(identb[:, :], identf))
            dve(lambda: e.memset(ones[:, :], 1.0))
            dve(lambda: e.memset(mhalf[:, :], -0.5))
            dve(lambda: e.memset(eps[:, :], 1e-5))
            dve(lambda: e.memset(zrow[:, :], 0.0))
            for who in ("sp", "pe", "ac", "pl", "dv"):
                sync(who, "V")
            if sp:
                for y in (ya, yb):
                    s_small.inc(e.dma_start(y.rearrange("(b n) c -> b n c", b=B)[:, 0, :], zrow[:, :]), 16)
            prep["small"] += 32
            if sp:
                loaded("small")

            def ln_pass(c):
                def body(n):
                    GG = GRP * c + n
                    T = U * n
                    if sp:
                        s_ln["dvXN"].wait(e, U * (GG + 1))
                        dst = ya[bass.ds(P * T + n // 2 + 1, U * P), :].rearrange("(u p) c -> p u c", p=P)
                        s_ln["sST"].inc(e.dma_start(dst, Y[:, bass.ds(T, U), P:D]), 16)
                    if dv:
                        if c == 0:
                            s_x.wait(e, 16 * GRP)
                        for u in range(U):
                            i = e.bn_stats(st[:, u, :], tile(X, T + u))
                        s_ln["dvST"].inc(i)
                        s_ln["dvST"].wait_alone(e, GG + 1, s_passed)
                        for u in range(U):
                            i = e.bn_aggr(mv[:, u, :], st[:, u, :])
                        s_ln["dvAG"].inc(i)
                        s_ln["plRV"].wait(e, 2 * GG + 2)
                        for u in range(U):
                            i = e.tensor_scalar(tile(Y, T + u), tile(X, T + u), mv[:, u, 0:1], rv[:, u:u + 1],
                                                ALU.subtract, ALU.mult)
                            s_ln["dvXN"].inc(i)
                    if pl:
                        s_ln["dvAG"].wait(e, GG + 1)
                        s_ln["plRV"].inc(e.tensor_tensor(rv[:, :], mv[:, :, 1], eps[:, 0:U], ALU.add))
                        s_ln["plRV"].wait(e, 2 * GG + 1)
                        s_ln["plRV"].inc(e.tensor_tensor(rv[:, :], rv[:, :], mhalf[:, 0:U], ALU.pow))

                if c == 0 and sp:
                    for n in range(GRP):
                        s_x.inc(e.dma_start(X[:, U * n:U * n + U, :], x_v[:, U * n:U * n + U, :]), 16)
                if dv or pl or sp:
                    loop(GRP, body)
                s_ln["dvXN"].wait(e, NT * (c + 1))
                if sp:
                    s_ln["sST"].wait(e, 16 * GRP * (c + 1))

            def loads_A(l):
                one = bass.ds(l, 1)
                load(raw[:, :].rearrange("p (k n) -> p k n", k=KD),
                     a["L0_ffn_wqkv"][one, :, :].rearrange("a (k p) n -> p (a k) n", p=P), "raw")
                load(raw2[:, 0:KI * D].rearrange("p (k n) -> p k n", k=KI),
                     a["L0_ffn_wo"][one, :, :].rearrange("a (k p) n -> p (a k) n", p=P), "raw2")
                for i, name in enumerate(("L0_ffn_q_scale", "L0_ffn_k_scale")):
                    load(scales[:, i * DH:(i + 1) * DH], a[name][one, :].to_broadcast([P, DH]), "small")

            def prep_A():
                if not sp:
                    loaded("raw")
                    loaded("raw2")
                    loaded("small")
                act(lambda: e.activation(flat(wq_h[:, :, :]), raw[:, :], ACT.Copy))
                act(lambda: e.activation(flat(wo_h[:, :, :]), raw2[:, 0:KI * D], ACT.Copy))
                for j in range(2):
                    sc_ = scales[:, j * DH:(j + 1) * DH]
                    c_, s_ = rot[:, 2 * j, :, :], rot[:, 2 * j + 1, :, :]
                    c0, s0 = rotc[:, 2 * j, :, :], rotc[:, 2 * j + 1, :, :]
                    dve(lambda: e.tensor_tensor(c_, c0, sc_.unsqueeze(1).to_broadcast([P, TB, DH]), ALU.mult))
                    hf = DH // 2
                    dve(lambda: e.tensor_tensor(s_[:, :, 0:hf], s0[:, :, 0:hf],
                                                sc_[:, hf:DH].unsqueeze(1).to_broadcast([P, TB, hf]), ALU.mult))
                    dve(lambda: e.tensor_tensor(s_[:, :, hf:DH], s0[:, :, hf:DH],
                                                sc_[:, 0:hf].unsqueeze(1).to_broadcast([P, TB, hf]), ALU.mult))
                sync("dv", "A")
                dve(lambda: e.tensor_tensor(flat(wq_l[:, :, :]), raw[:, :], flat(wq_h[:, :, :]).bitcast(F32), ALU.subtract))
                dve(lambda: e.tensor_tensor(flat(wo_l[:, :, :]), raw2[:, 0:KI * D], flat(wo_h[:, :, :]).bitcast(F32), ALU.subtract))
                dve(lambda: e.memset(kTh[:, :, :, :].bitcast(F32), 0.0))
                dve(lambda: e.memset(kTl[:, :, :, :].bitcast(F32), 0.0))
                dve(lambda: e.memset(V[U - 1][:, :], 0.0))
                dve(lambda: e.tensor_copy(mask0[:, :], maskE))
                for who in ("pe", "ac", "pl", "dv", "sp"):
                    sync(who, "A", "V")

            def pipeline(order, steps, extra=None):
                mine = []
                for word in order[E].split():
                    cut = max(word.rfind("+"), word.rfind("-"))
                    mine.append((steps[word[:cut]], int(word[cut:])))
                lead = max([k for _, k in mine], default=0)
                lag = -min([k for _, k in mine], default=0)

                def slot(T, u, known):
                    for f, k in mine:
                        if not known or 0 <= T + k < NT:
                            f(T + k, (u + k) % U)

                def iteration(it, known):
                    for u in range(U):
                        slot(U * it + u, u, known)
                        if extra:
                            extra(it, u)

                assert lead <= U and lag <= U
                for T in range(-lead, 0):
                    slot(T, T % U, True)
                iteration(0, True)
                if mine or extra:
                    loop(NIT - 2, lambda i: iteration(i + 1, False))
                iteration(NIT - 1, True)
                for T in range(NT, NT + lag):
                    slot(T, T % U, True)

            def before(T):
                return min(T, NT - 1) if isinstance(T, int) else T

            def attn_steps(run):
                R0 = NT * run

                def ld(T, u):
                    if sp:
                        s["peHT"].wait(e, R0 + T - (U - 1))
                        row = P * T + (T // TB)
                        s_ld[u].inc(e.dma_start(H[u][:, 0:P], tile(Y, T)[:, 0:P]), 16)
                        s_ld[u].inc(e.dma_start(H[u][:, P:D], ya[bass.ds(row, P), :]), 16)

                def ht(T, u):
                    if pe:
                        s_ld[u].wait(e, 32 * ((R0 + T - u) // U + 1))
                        s["acSQ"].wait(e, 2 * (R0 + T))
                        s["dvRT"].wait(e, 4 * (R0 + T))
                        e.transpose(bank[1][:, 0:P], H[u][:, 0:P], identf)
                        s["peHT"].inc(e.transpose(bank[1][:, P:D], H[u][:, P:D], identf))
                    if ac:
                        s["peHT"].wait(e, R0 + T + 1)
                        s["acHT"].inc(e.activation(hTh[u % 2][:, :], bank[1][:, 0:D], ACT.Copy))
                    if dv:
                        s["acHT"].wait(e, R0 + T + 1)
                        s["dvHT"].inc(e.tensor_tensor(hTl[u % 2][:, :], bank[1][:, 0:D],
                                                      hTh[u % 2][:, :].bitcast(F32), ALU.subtract))

                def proj(o, u, c0, n):
                    for k in range(KD):
                        w = (slice(None), k, slice(c0, c0 + n))
                        lt = slice(k * P, (k + 1) * P)
                        i = three(o, hTh[u % 2][:, lt], hTl[u % 2][:, lt], wq_h[w], wq_l[w], k == 0, k == KD - 1)
                    return i

                def heads(x):
                    return x.rearrange("p (h d) -> p h d", h=HEADS)

                def half(u, j):
                    return qk[u % 2][:, j * INNER:(j + 1) * INNER]

                def qk_(T, u, j):
                    G = R0 + T
                    if pe:
                        s["dvHT"].wait(e, G + 1)
                        s["dvKT"].wait(e, 2 * (G - 2) + j + 1)
                        s["peQK"].inc(proj(bank[j][:, :], u, INNER * j, INNER))
                    if ac:
                        s["peQK"].wait(e, 2 * G + j + 1)
                        s["acSQ"].inc(e.activation(half(u, j), bank[j][:, :], ACT.Square))
                    if dv:
                        s["acSQ"].wait(e, 2 * G + j + 1)
                        s["plAD"].wait(e, 2 * (G - 1) + j + 1)
                        o1_, o2_ = heads(t1[:, j * INNER:(j + 1) * INNER]), heads(t2[:, j * INNER:(j + 1) * INNER])
                        x_ = heads(bank[j][:, :])
                        hf = DH // 2

                        def tab(i, lo, hi):
                            return rot_at(i, T)[:, lo:hi].unsqueeze(1).to_broadcast([P, HEADS, hi - lo])

                        s["dvRT"].inc(e.tensor_tensor(o1_, x_, tab(2 * j, 0, DH), ALU.mult))
                        e.tensor_tensor(o2_[:, :, 0:hf], x_[:, :, hf:DH], tab(2 * j + 1, 0, hf), ALU.mult)
                        s["dvRT"].inc(e.tensor_tensor(o2_[:, :, hf:DH], x_[:, :, 0:hf], tab(2 * j + 1, hf, DH), ALU.mult))

                def rot_at(i, T):
                    pos = T - TB * (T // TB)
                    if isinstance(pos, int):
                        return rot[:, i, pos, :]
                    return flat(rot[:, i, bass.ds(nc.s_assert_within(
                        pos, 0, TB - 1, skip_runtime_bounds_check_because="the remainder of a division by TB"), 1), :])

                def sum_(T, u, j):
                    G = R0 + T
                    if dv:
                        s["acSQ"].wait(e, 2 * G + j + 1)
                        s["dvSS"].inc(e.tensor_reduce(ss[:, j * HEADS:(j + 1) * HEADS], heads(half(u, j)), AX.X, ALU.add))
                        if j == 1:
                            s["dvSS"].wait(e, 3 * G + 2)
                            s["dvSS"].inc(e.tensor_scalar(ss[:, :], ss[:, :], 1e-24, None, ALU.max))
                    if pl and j == 1:
                        s["dvSS"].wait(e, 3 * G + 3)
                        s["plRN"].inc(e.tensor_tensor(rn[:, :], ss[:, :], mhalf[:, :], ALU.pow))

                def add_(T, u, j):
                    G = R0 + T
                    if pl:
                        s["dvSS"].wait(e, 3 * G + j + 1)
                        s["dvRT"].wait(e, 4 * G + 2 * j + 2)
                        w = slice(j * INNER, (j + 1) * INNER)
                        s["plAD"].inc(e.tensor_tensor(half(u, j), t1[:, w], t2[:, w], ALU.add))

                def norm_(T, u, j):
                    G = R0 + T
                    if dv:
                        s["plRN"].wait(e, G + 1)
                        s["plAD"].wait(e, 2 * G + j + 1)
                        s["dvQN"].inc(e.tensor_tensor(
                            heads(half(u, j)), heads(half(u, j)),
                            rn[:, j * HEADS:(j + 1) * HEADS].unsqueeze(2).to_broadcast([P, HEADS, DH]), ALU.mult))

                def v_(T, u):
                    G = R0 + T
                    if pe:
                        s["acSQ"].wait(e, 2 * G + 1)
                        s["dvRT"].wait(e, 4 * G + 2)
                        s["peV"].inc(proj(bank[0][:, :], u, 2 * INNER, INNER))
                    if ac:
                        s["peV"].wait(e, G + 1)
                        s["acV"].inc(e.activation(V[u][:, :], bank[0][:, :], ACT.Copy))

                def tr_(T, u, j):
                    G = R0 + T
                    r = u % 2
                    hi = qTh[r][:, :] if j == 0 else kTh[:, :, r, :]
                    lo = qTl[r][:, :] if j == 0 else kTl[:, :, r, :]
                    src = bank[j][:, :] if j == 0 else bank[j][:, :].rearrange("p (c k) -> p c k", c=KI)
                    if pe:
                        s["dvQN"].wait(e, 2 * G + j + 1)
                        if j == 0:
                            s["acV"].wait(e, R0 + before(T + 1) + 1)
                        else:
                            s["dvHT"].wait(e, R0 + before(T + 2) + 1)
                        for c in range(KI):
                            i = e.transpose(bank[j][:, c * P:(c + 1) * P], half(u, j)[:, c * P:(c + 1) * P], identf)
                        s["peKT"].inc(i)
                    if ac:
                        s["peKT"].wait(e, 2 * G + j + 1)
                        s["acKT"].inc(e.activation(hi, src, ACT.Copy))
                    if dv:
                        s["acKT"].wait(e, 2 * G + j + 1)
                        s["dvKT"].inc(e.tensor_tensor(lo, src, hi.bitcast(F32), ALU.subtract))

                def sc_(T, u, gi):
                    G = R0 + T
                    r = u % 2
                    n = NG * G + gi
                    bk = bank[2 + gi % 2]
                    hs = PAIRS[gi]
                    if pe:
                        s["dvKT"].wait(e, 2 * G + 2)
                        s["acEX"].wait(e, n - 1)
                        if u == 0:
                            s["plM0"].wait(e, GRP * run + T // U + 1)
                        m = mask0[:, :] if u == 0 else (maskE if r == 0 else maskO)
                        e.matmul(bk[:, :], identb[:, :], m, start=True, stop=False, skip_group_check=True)
                        for i, h in enumerate(hs):
                            pp = slice(DH * (h % 2), DH * (h % 2) + DH)
                            c = h // 2
                            o, lt = bk[:, i * 256:(i + 1) * 256], slice(c * P, (c + 1) * P)
                            kh, kl = (x[pp, c, :, :].rearrange("p a k -> p (a k)") for x in (kTh, kTl))
                            e.matmul(o, qTh[r][pp, lt], kh, start=False, stop=False, skip_group_check=True)
                            e.matmul(o, qTh[r][pp, lt], kl, start=False, stop=False, skip_group_check=True)
                            ins = e.matmul(o, qTl[r][pp, lt], kh, start=False, stop=True, skip_group_check=True)
                        s["peS"].inc(ins)
                    if dv:
                        s["peS"].wait(e, n + 1)
                        s["dvMX"].inc(e.tensor_reduce(nm[r][:, 2 * gi:2 * gi + 2],
                                                      bk[:, :].rearrange("p (h k) -> p h k", h=2), AX.X, ALU.max, negate=True))
                    if ac:
                        s["dvMX"].wait(e, n + 1)
                        s["pePT"].wait(e, n - 1)
                        for i, h in enumerate(hs):
                            ins = e.activation(Pb[gi % 2][:, i * 256:(i + 1) * 256], bk[:, i * 256:(i + 1) * 256], ACT.Exp,
                                               bias=nm[r][:, 2 * gi + i:2 * gi + i + 1], accum_out=sums[r][:, h:h + 1])
                        s["acEX"].inc(ins)

                def pt_(T, u, gi):
                    n = NG * (R0 + T) + gi
                    b_ = bank[4 + gi % 2]
                    if pe:
                        s["acEX"].wait(e, n + 1)
                        s["acPT"].wait(e, n - 1)
                        for x in range(4):
                            i = e.transpose(b_[:, x * P:(x + 1) * P], Pb[gi % 2][:, x * P:(x + 1) * P], identf)
                        s["pePT"].inc(i)
                    if ac:
                        s["pePT"].wait(e, n + 1)
                        s["pePV"].wait(e, n - 1)
                        s["acPT"].inc(e.activation(PTs[gi % 2][:, :], b_[:, :], ACT.Copy))

                def pv_(T, u, gi):
                    G = R0 + T
                    n = NG * G + gi
                    if pe:
                        s["acPT"].wait(e, n + 1)
                        if gi == 0:
                            s["acV"].wait(e, G + 1)
                            s["dvON"].wait(e, G)
                        for i, h in enumerate(PAIRS[gi]):
                            for kt in range(2):
                                vt = V[u] if u % 2 == kt else V[(u - 1) % U]
                                ins = e.matmul(bank[6][:, h * DH:(h + 1) * DH],
                                               PTs[gi % 2][:, (2 * i + kt) * P:(2 * i + kt + 1) * P],
                                               vt[:, h * DH:(h + 1) * DH], start=(kt == 0), stop=(kt == 1))
                        s["pePV"].inc(ins)

                def rs_(T, u):
                    if dv:
                        s["acEX"].wait(e, NG * (R0 + T) + NG)
                        s["dvRS"].inc(e.reciprocal(rs[:, :], sums[u % 2][:, :]))

                def on_(T, u):
                    G = R0 + T
                    if dv:
                        s["dvRS"].wait(e, G + 1)
                        s["pePV"].wait(e, NG * G + NG)
                        s["peOT"].wait(e, G)
                        s["dvON"].inc(e.tensor_tensor(heads(On[:, :]), heads(bank[6][:, :]),
                                                      rs[:, :].unsqueeze(2).to_broadcast([P, HEADS, DH]), ALU.mult))

                def ot_(T, u):
                    G = R0 + T
                    if pe:
                        s["dvON"].wait(e, G + 1)
                        s["dvY"].wait(e, G)
                        for c in range(KI):
                            i = e.transpose(bank[7][:, c * P:(c + 1) * P], On[:, c * P:(c + 1) * P], identf)
                        s["peOT"].inc(i)
                    if ac:
                        s["peOT"].wait(e, G + 1)
                        s["acOT"].inc(e.activation(OTh[:, :], bank[7][:, :], ACT.Copy))
                    if dv:
                        s["acOT"].wait(e, G + 1)
                        s["dvOT"].inc(e.tensor_tensor(OTl[:, :], bank[7][:, :], OTh[:, :].bitcast(F32), ALU.subtract))

                def wo_(T, u):
                    G = R0 + T
                    if pe:
                        s["dvOT"].wait(e, G + 1)
                        for c in range(KI):
                            lt = slice(c * P, (c + 1) * P)
                            i = three(bank[7][:, 0:D], OTh[:, lt], OTl[:, lt], wo_h[:, c, :], wo_l[:, c, :], c == 0, c == KI - 1)
                        s["peWO"].inc(i)
                    if dv:
                        s["peWO"].wait(e, G + 1)
                        s["dvY"].inc(e.tensor_tensor(tile(Y, T), bank[7][:, 0:D], tile(Y, T), ALU.add))
                    if sp:
                        s["dvY"].wait(e, G + 1)
                        row = P * T + (T // TB) + 1
                        s_st[u].inc(e.dma_start(yb[bass.ds(row, P), :], tile(Y, T)[:, P:D]), 16)

                def by(step_, i):
                    return lambda T, u: step_(T, u, i)

                f = {"ld": ld, "ht": ht, "v": v_, "rs": rs_, "on": on_, "ot": ot_, "wo": wo_}
                for j, name in enumerate("qk"):
                    f.update({name: by(qk_, j), "sum_" + name: by(sum_, j), "add_" + name: by(add_, j),
                              "norm_" + name: by(norm_, j), name + "T": by(tr_, j)})
                for gi in range(NG):
                    f.update({f"sc{gi}": by(sc_, gi), f"pt{gi}": by(pt_, gi), f"pv{gi}": by(pv_, gi)})
                return f

            def pass_A(run):
                def mask_of(it):
                    s["peS"].wait(e, NG * (NT * run + U * it - U) + NG)
                    for x in range(2):
                        i = e.tensor_copy(mask0[:, 256 * x + P:256 * x + 2 * P],
                                          masksel[:, bass.ds(it, 1), :].rearrange("p a k -> p (a k)"))
                    s["plM0"].inc(i)

                def next_mask(it, u):
                    if u == 1 and not (isinstance(it, int) and it == NIT - 1):
                        mask_of(it + 1)

                if pl:
                    mask_of(0)
                pipeline(ATTN, attn_steps(run), next_mask if pl else None)
                s["dvY"].wait(e, NT * (run + 1))
                if sp:
                    for x in s_st:
                        x.wait(e, 16 * GRP * (run + 1))

            def loads_B(l):
                one = bass.ds(l, 1)
                W1 = raw[:, 0:KD * 2 * HID].rearrange("p (k n) -> p k n", k=KD)
                load(W1, a["L0_ffn_w1"][one, :, :].rearrange("a (k p) n -> p (a k) n", p=P), "raw")
                W2 = raw2[:, 0:CH * D].rearrange("p (k n) -> p k n", k=CH)
                load(W2[:, 0:CH - 1, :], a["L0_ffn_w2"][one, 0:(CH - 1) * P, :].rearrange("a (k p) n -> p (a k) n", p=P), "raw2")
                load(W2[0:HTAIL, CH - 1, :], a["L0_ffn_w2"][one, (CH - 1) * P:HID, :].rearrange("a p n -> (a p) n"), "raw2")
                load(vec[:, 0:KD], a["L0_ffn_ln_g"][one, :].rearrange("a (k p) -> p (a k)", p=P), "small", True)
                load(vec[:, 4:4 + KD], a["L0_ffn_ln_b"][one, :].rearrange("a (k p) -> p (a k)", p=P), "small", True)
                b1 = a["L0_ffn_b1"]
                for j in range(2):
                    load(bias1[:, j * CH:j * CH + CH - 1],
                         b1[one, j * HID:j * HID + (CH - 1) * P].rearrange("a (k p) -> p (a k)", p=P), "small", True)
                    r0 = TAILG * j
                    load(bias1[r0:r0 + HTAIL, j * CH + CH - 1:j * CH + CH],
                         b1[one, j * HID + (CH - 1) * P:(j + 1) * HID].rearrange("a p -> p a"), "small", True)
                load(brow[:, :], a["L0_ffn_b2"][one, :].to_broadcast([P, D]), "small")

            def prep_B():
                W1 = raw[:, 0:KD * 2 * HID].rearrange("p (k n) -> p k n", k=KD)
                W2 = raw2[:, 0:CH * D].rearrange("p (k n) -> p k n", k=CH)
                if not sp:
                    loaded("raw")
                    loaded("raw2")
                    loaded("small")
                sync("pe", "V")
                tail = (CH - 1) * P
                for j in range(2):
                    for c in range(CH):
                        m = P if c < CH - 1 else HTAIL
                        r0 = TAILG * j if c == CH - 1 else 0
                        for k in range(KD):
                            col = j * HID + c * P
                            tens(lambda: e.matmul(bank[0][r0:r0 + m, j * CH + c:j * CH + c + 1],
                                                  W1[:, k, col:col + m], vec[:, 4 + k:5 + k],
                                                  start=(k == 0), stop=(k == KD - 1)))
                sync("dv", "P")
                for j in range(2):
                    w = slice(j * CH, j * CH + CH - 1)
                    dve(lambda: e.tensor_tensor(bias1[:, w], bias1[:, w], bank[0][:, w], ALU.add))
                    r = slice(TAILG * j, TAILG * j + HTAIL)
                    w2_ = slice(j * CH + CH - 1, j * CH + CH)
                    dve(lambda: e.tensor_tensor(bias1[r, w2_], bias1[r, w2_], bank[0][r, w2_], ALU.add))
                for k in range(KD):
                    dve(lambda: e.tensor_scalar(W1[:, k, :], W1[:, k, :], vec[:, k:k + 1], None, ALU.mult))
                sync("ac", "V")
                main = (CH - 1) * P
                pieces = [(0, 0, main), (main, HID, main), (2 * main, main, HTAIL), (2 * main + TAILG, HID + main, HTAIL)]
                dve(lambda: e.memset(w1_h[:, :, 2 * main:].bitcast(F32), 0.0))
                dve(lambda: e.memset(w1_l[:, :, 2 * main:].bitcast(F32), 0.0))
                sync("ac", "V")
                for d0, s0, n in pieces:
                    act(lambda: e.activation(w1_h[:, :, d0:d0 + n], W1[:, :, s0:s0 + n], ACT.Copy))
                act(lambda: e.activation(w2_h[:, 0:CH - 1, :], W2[:, 0:CH - 1, :], ACT.Copy))
                act(lambda: e.activation(w2_h[0:HTAIL, CH - 1, :], W2[0:HTAIL, CH - 1, :], ACT.Copy))
                sync("dv", "A", "V")
                for d0, s0, n in pieces:
                    dve(lambda: e.tensor_tensor(w1_l[:, :, d0:d0 + n], W1[:, :, s0:s0 + n],
                                                w1_h[:, :, d0:d0 + n].bitcast(F32), ALU.subtract))
                dve(lambda: e.tensor_tensor(w2_l[:, 0:CH - 1, :], W2[:, 0:CH - 1, :],
                                            w2_h[:, 0:CH - 1, :].bitcast(F32), ALU.subtract))
                dve(lambda: e.tensor_tensor(w2_l[0:HTAIL, CH - 1, :], W2[0:HTAIL, CH - 1, :],
                                            w2_h[0:HTAIL, CH - 1, :].bitcast(F32), ALU.subtract))
                for who in ("pe", "ac", "pl", "dv", "sp"):
                    sync(who, "A", "V", "P")

            def ternary(W):
                dve(lambda: e.tensor_reduce(thr[:, 0:1], W, AX.X, ALU.add, apply_absolute_value=True))
                sync("pe", "V")
                tens(lambda: e.matmul(bank[0][:, 0:1], ones[:, :], thr[:, 0:1], start=True, stop=True))
                sync("dv", "P")
                dve(lambda: e.tensor_scalar(thr[:, 1:2], bank[0][:, 0:1], 1.0 / (FF * D), 1e-5, ALU.mult, ALU.add))
                sync("dv", "V")
                dve(lambda: e.tensor_scalar(thr[:, 2:3], thr[:, 1:2], 0.5, None, ALU.mult))
                dve(lambda: e.tensor_scalar(thr[:, 3:4], thr[:, 1:2], -0.5, None, ALU.mult))
                sync("dv", "V")
                neg = Y[:, 0:TB, :].rearrange("p t c -> p (t c)")
                dve(lambda: e.tensor_scalar(neg, W, thr[:, 3:4], None, ALU.is_lt))
                dve(lambda: e.tensor_scalar(W, W, thr[:, 2:3], None, ALU.is_gt))
                sync("dv", "V")
                dve(lambda: e.tensor_tensor(W, W, neg, ALU.subtract))

            def loads_F():
                load(raw[:, 0:CF * D].rearrange("p (c n) -> p c n", c=CF), a["L1_ffn_W1"].rearrange("(c p) n -> p c n", p=P), "raw")
                load(raw2[:, :].rearrange("p (c n) -> p c n", c=KD), a["L1_ffn_W2"].rearrange("(c p) n -> p c n", p=P), "raw2")

            def prep_F():
                Wa, Wb = raw[:, 0:CF * D], raw2[:, 0:2048]
                load(bias1[:, 0:CF], a["L1_ffn_b1"].rearrange("(c p) -> p c", p=P), "small", True)
                load(brow[:, :], a["L1_ffn_b2"].rearrange("(a n) -> a n", a=1).to_broadcast([P, D]), "small")
                if not sp:
                    loaded("raw")
                    loaded("raw2")
                    loaded("small")
                ternary(Wa)
                ternary(Wb)
                sync("pe", "V")
                for c in range(CF):
                    for k in range(KD):
                        tens(lambda: e.transpose(bank[c // 2][:, (2 * (c % 2) + k) * P:(2 * (c % 2) + k + 1) * P],
                                                 Wa[:, c * D + k * P:c * D + (k + 1) * P], identf))
                for k in range(KD):
                    for c in range(CF):
                        tens(lambda: e.transpose(bank[4 + c // 2][:, (2 * (c % 2) + k) * P:(2 * (c % 2) + k + 1) * P],
                                                 Wb[:, k * FF + c * P:k * FF + (c + 1) * P], identf))
                sync("dv", "P")
                for c in range(CF):
                    src = bank[c // 2][:, 2 * (c % 2) * P:2 * (c % 2) * P + D]
                    dve(lambda: e.tensor_copy(w1_h[:, :, c * P:(c + 1) * P], src.rearrange("p (k f) -> p k f", k=KD)))
                    src2 = bank[4 + c // 2][:, 2 * (c % 2) * P:2 * (c % 2) * P + D]
                    dve(lambda: e.tensor_copy(w2_h[:, c, :], src2))
                dve(lambda: e.tensor_scalar(brow[:, :], brow[:, :], 0.5, None, ALU.mult))
                for who in ("pe", "ac", "pl", "dv", "sp"):
                    sync(who, "A", "V", "P")

            def ffn(pas, cb, l0, final=False):
                nch = CH if l0 else CF
                G0 = GRP * pas
                R = Y if l0 else X

                def loadh(n):
                    if sp and l0:
                        s["dvXN"].wait(e, U * (G0 + n))
                        T = U * n
                        s["sHB"].inc(e.dma_start(HB[:, :, 0:P], Y[:, bass.ds(T, U), 0:P]), 16)
                        src = yb[bass.ds(P * T + n // 2, U * P), :].rearrange("(u p) c -> p u c", p=P)
                        s["sHB"].inc(e.dma_start(HB[:, :, P:D], src), 16)

                def hb(n):
                    s["sHB"].wait(e, 32 * (G0 + n + 1))

                def src(n, u):
                    return HB[:, u, :] if l0 else tile(X, U * n + u)

                def ln1(n):
                    G = G0 + n
                    if dv:
                        if l0:
                            hb(n)
                        for u in range(U):
                            i = e.bn_stats(st[:, u, :], src(n, u))
                        s["dvST"].inc(i)
                        s["dvST"].wait_alone(e, G + 1, s_passed)
                        for u in range(U):
                            i = e.bn_aggr(mv[:, u, :], st[:, u, :])
                        s["dvAG"].inc(i)
                    if pl:
                        s["dvAG"].wait(e, G + 1)
                        s["plRV"].inc(e.tensor_tensor(rv[:, :], mv[:, :, 1], eps[:, 0:U], ALU.add))
                        s["plRV"].wait(e, 2 * G + 1)
                        s["plRV"].inc(e.tensor_tensor(rv[:, :], rv[:, :], mhalf[:, 0:U], ALU.pow))

                def ln2(n):
                    G = G0 + n
                    if dv:
                        s["plRV"].wait(e, 2 * G + 2)
                        s["peTR"].wait(e, 2 * G)
                        for u in range(U):
                            s["dvXN"].inc(e.tensor_scalar(Xn[:, u, :], src(n, u), mv[:, u, 0:1], rv[:, u:u + 1],
                                                          ALU.subtract, ALU.mult))
                    if pl:
                        if l0:
                            hb(n)
                        else:
                            s["dvXN"].wait(e, U * G + U)
                        v = R[:, bass.ds(U * n, U), :]
                        s["plB2"].inc(e.tensor_tensor(v, v, brow[:, :].unsqueeze(1).to_broadcast([P, U, D]), ALU.add))

                def tr(n):
                    G = G0 + n
                    if pe:
                        s["dvXN"].wait(e, U * G + U)
                        s["dvLO"].wait(e, 2 * G)
                        for k in range(KD):
                            for u in range(U):
                                i = e.transpose(bank[k][:, u * P:(u + 1) * P], Xn[:, u, k * P:(k + 1) * P], identf)
                            s["peTR"].inc(i)
                    for k in range(KD):
                        if ac:
                            s["peTR"].wait(e, 2 * G + k + 1)
                            s["acHI"].inc(e.activation(gTh[:, k, :], bank[k][:, :], ACT.Copy))
                        if dv:
                            s["acHI"].wait(e, 2 * G + k + 1)
                            s["dvLO"].inc(e.tensor_tensor(gTl[:, k, :], bank[k][:, :], gTh[:, k, :].bitcast(F32), ALU.subtract))

                def w1mm(o, col):
                    for k in range(KD):
                        w = (slice(None), k, slice(col, col + P))
                        if l0:
                            i = three(o, w1_h[w], w1_l[w], gTh[:, k, :], gTl[:, k, :], k == 0, k == KD - 1)
                        else:
                            e.matmul(o, w1_h[w], gTh[:, k, :], start=(k == 0), stop=False)
                            i = e.matmul(o, w1_h[w], gTl[:, k, :], start=False, stop=(k == KD - 1))
                    return i

                def piece(n, c):
                    ci = cb + nch * n + c
                    G = G0 + n
                    bg, ba = bank[2 + 2 * (c % 2)], bank[3 + 2 * (c % 2)]
                    p2 = c % 2
                    tail = l0 and c == CH - 1
                    m = HTAIL if tail else P
                    gp = slice(TAILG, TAILG + HTAIL) if tail else slice(0, P)
                    if pe:
                        if c == 0:
                            s["dvLO"].wait(e, 2 * G + 2)
                        s["dvHD" if l0 else "acU"].wait(e, ci - 1)
                        if l0:
                            s["peG"].inc(w1mm(bg[:, :], (CH - 1) * P + c * P))
                            if not tail:
                                s["peA"].inc(w1mm(ba[:, :], c * P))
                        else:
                            s["peG"].inc(w1mm(bg[:, :], c * P))
                    if l0:
                        if ac:
                            s["peG"].wait(e, ci + 1)
                            s["dvHD"].wait(e, ci - 1)
                            s["acU"].inc(e.activation(gate[p2][0:m, :], bg[gp, :], ACT.Gelu, bias=bias1[gp, CH + c:CH + c + 1]))
                        if dv:
                            s["acU"].wait(e, ci + 1)
                            if not tail:
                                s["peA"].wait(e, (CH - 1) * G + c + 1)
                            s["dvHD"].inc(e.scalar_tensor_tensor(hid[p2][0:m, :], (bg if tail else ba)[0:m, :],
                                                                 bias1[0:m, c:c + 1], gate[p2][0:m, :], ALU.add, ALU.mult))
                            s["dvHD"].wait(e, ci + 1)
                            s["peW2"].wait(e, U * G)
                            s["xxHH"].inc(e.tensor_copy(hidh[0:m, c, :], hid[p2][0:m, :]))
                    else:
                        if ac:
                            s["peG"].wait(e, ci + 1)
                            s["dvHL"].wait(e, ci - 1)
                            s["acU"].inc(e.activation(hid[p2][:, :], bg[:, :], ACT.Relu, bias=bias1[:, c:c + 1]))
                            s["acU"].wait(e, ci + 1)
                            s["peW2"].wait(e, U * G)
                            s["xxHH"].inc(e.activation(hidh[:, c, :], hid[p2][:, :], ACT.Copy))
                    if dv:
                        s["xxHH"].wait(e, ci + 1)
                        if not l0:
                            s["peW2"].wait(e, U * G)
                        s["dvHL"].inc(e.tensor_tensor(hidl[0:m, c, :], hid[p2][0:m, :], hidh[0:m, c, :].bitcast(F32), ALU.subtract))

                def w2_(n):
                    G = G0 + n
                    for u in range(U):
                        i_ = U * G + u
                        o = bank[6 + u % 2][:, 0:D]
                        if pe:
                            s["dvYB"].wait(e, i_ - 1)
                            for c in range(nch):
                                m = HTAIL if (l0 and c == CH - 1) else P
                                if u == 0:
                                    s["dvHL"].wait(e, cb + nch * n + c + 1)
                                lt = slice(u * P, (u + 1) * P)
                                if l0:
                                    i = three(o, hidh[0:m, c, lt], hidl[0:m, c, lt], w2_h[0:m, c, :], w2_l[0:m, c, :],
                                              c == 0, c == nch - 1)
                                else:
                                    e.matmul(o, hidh[:, c, lt], w2_h[:, c, :], start=(c == 0), stop=False)
                                    i = e.matmul(o, hidl[:, c, lt], w2_h[:, c, :], start=False, stop=(c == nch - 1))
                            s["peW2"].inc(i)
                        if dv:
                            s["peW2"].wait(e, i_ + 1)
                            if u == 0:
                                s["plB2"].wait(e, G + 1)
                            v = tile(R, U * n + u)
                            if l0:
                                s["dvYB"].inc(e.tensor_tensor(v, o, v, ALU.add))
                            else:
                                s["dvYB"].inc(e.scalar_tensor_tensor(v, o, 0.5, v, ALU.mult, ALU.add))
                    if sp and (l0 or final):
                        s["dvYB"].wait(e, U * G + U)
                        T = U * n
                        if l0:
                            dst = ya[bass.ds(P * T + n // 2 + 1, U * P), :].rearrange("(u p) c -> p u c", p=P)
                            s_stb.inc(e.dma_start(dst, Y[:, bass.ds(T, U), P:D]), 16)
                        else:
                            s_stb.inc(e.dma_start(out_v[:, bass.ds(T, U), :], X[:, bass.ds(T, U), :]), 16)

                def group(n, last):
                    if not last:
                        loadh(n + 1)
                    for c in range(nch):
                        piece(n, c)
                        if c == 1 and not last:
                            ln1(n + 1)
                        if c == 3 and not last:
                            ln2(n + 1)
                    if not last:
                        tr(n + 1)
                    w2_(n)

                loadh(0)
                ln1(0)
                ln2(0)
                tr(0)
                group(0, False)
                loop(GRP - 2, lambda i: group(i + 1, False))
                group(GRP - 1, True)
                s["dvYB"].wait(e, U * (G0 + GRP))
                if (sp or dv) and l0:
                    s_stb.wait(e, 16 * (G0 + GRP))
                if sp and final:
                    s_stb.wait(e, 16 * GRP * (NRUN + 1))

            def merge(c):
                if dv:
                    def body(n):
                        v, w = X[:, bass.ds(U * n, U), :], Y[:, bass.ds(U * n, U), :]
                        s["mdvY"].inc(e.scalar_tensor_tensor(flat(v), flat(w), 0.5, flat(v), ALU.mult, ALU.add))
                    loop(GRP, body)
                s["mdvY"].wait(e, GRP * (c + 1))

            def loads_lin():
                load(wa, a["L0_attn_w_attn"].rearrange("(k p) n -> p k n", p=P), "raw")
                load(wp, a["L0_attn_w_proj"].rearrange("(k p) n -> p k n", p=P), "raw")

            def linear_attention():
                if not sp:
                    loaded("raw")
                for i in range(2):
                    pool(lambda: e.memset(qkp[i][:, :, :, :], 0.0))
                    pool(lambda: e.memset(va[i][:, :, :], 1.0))
                pool(lambda: e.memset(Sbd[:, :, :], 0.0))
                for who in ("pe", "ac", "dv"):
                    sync(who, "B")
                causal = misc[:, MC:MC + P]
                blk = misc[:, MB:MB + 4 * VA]

                def ln1(T, u):
                    r = u % 2
                    if dv:
                        z["dvST"].inc(e.bn_stats(st0[:, r, :], tile(X, T)))
                        z["dvST"].wait_alone(e, T + 1, s_passed)
                        z["dvAG"].inc(e.bn_aggr(mv0[:, r, :], st0[:, r, :]))
                    if pl:
                        z["dvAG"].wait(e, T + 1)
                        z["plRV"].inc(e.tensor_tensor(rv0[:, r:r + 1], mv0[:, r, 1:2], eps[:, 0:1], ALU.add))
                        z["plRV"].wait(e, 2 * T + 1)
                        z["plRV"].inc(e.tensor_tensor(rv0[:, r:r + 1], rv0[:, r:r + 1], mhalf[:, 0:1], ALU.pow))

                def ln2(T, u):
                    r = u % 2
                    if dv:
                        z["plRV"].wait(e, 2 * T + 2)
                        z["peTR"].wait(e, T - 1)
                        z["dvXN"].inc(e.tensor_scalar(Xn0[r][:, :], tile(X, T), mv0[:, r, 0:1], rv0[:, r:r + 1],
                                                      ALU.subtract, ALU.mult))

                def tr(T, u):
                    r = u % 2
                    if pe:
                        z["dvXN"].wait(e, T + 1)
                        z["dvDL"].wait(e, T - 1)
                        z["acHT"].wait(e, T)
                        for k in range(KD):
                            i = e.transpose(bank[0][:, k * P:(k + 1) * P], Xn0[r][:, k * P:(k + 1) * P], identf)
                        z["peTR"].inc(i)
                    if ac:
                        z["peTR"].wait(e, T + 1)
                        z["acHT"].inc(e.activation(h0[r][:, :], bank[0][:, 0:D], ACT.Copy))

                def qkv(T, u):
                    r = u % 2
                    if pe:
                        z["acHT"].wait(e, T + 1)
                        z["dvQK"].wait(e, T)
                        z["dvX"].wait(e, T - 2)
                        for k in range(KD):
                            i = e.matmul(bank[1][:, :], h0[r][:, k * P:(k + 1) * P], wa[:, k, 0:2 * D],
                                         start=(k == 0), stop=(k == KD - 1))
                        z["peQK"].inc(i)
                        for k in range(KD):
                            i = e.matmul(bank[2][:, 0:D], h0[r][:, k * P:(k + 1) * P], wa[:, k, 2 * D:3 * D],
                                         start=(k == 0), stop=(k == KD - 1))
                        z["peV"].inc(i)
                    if dv:
                        z["peQK"].wait(e, T + 1)
                        z["acEX"].wait(e, T)
                        z["dvMN"].inc(e.tensor_scalar(mn[:, :], bank[1][:, :], 0.0, None, ALU.min))
                    if ac:
                        z["dvMN"].wait(e, T + 1)
                        z["dvQK"].wait(e, T)
                        z["acEX"].inc(e.activation(ex[:, :], mn[:, :], ACT.Exp))
                        z["peV"].wait(e, T + 1)
                        z["peNU"].wait(e, T - 1)
                        z["acV"].inc(e.activation(va[r][:, :, 0:D0], bank[2][:, 0:D].rearrange("p (h d) -> p h d", h=H0),
                                                  ACT.Copy))

                def feat(T, u):
                    r = u % 2
                    if dv:
                        z["acEX"].wait(e, T + 1)
                        z["peDL"].wait(e, T - 1)
                        z["peTQ"].wait(e, 2 * T - 2)
                        z["dvQK"].inc(e.scalar_tensor_tensor(
                            qkp[r][:, :, :, 0:D0].rearrange("p a h d -> p (a h) d"),
                            bank[1][:, :].rearrange("p (x d) -> p x d", d=D0), 0.0,
                            ex[:, :].rearrange("p (x d) -> p x d", d=D0), ALU.max, ALU.add))

                def tq(T, u):
                    r = u % 2
                    if pe:
                        z["dvQK"].wait(e, T + 1)
                        z["dvAT"].wait(e, 4 * T)
                        for j in range(2):
                            v = qkp[r][:, j, :, :].rearrange("p h d -> p (h d)")
                            for c in range(4):
                                i = e.transpose(bank[4 + j][:, c * P:(c + 1) * P], v[:, c * P:(c + 1) * P], identf)
                            z["peTQ"].inc(i)
                    if ac:
                        for j, dst in enumerate((qT0, kT0)):
                            z["peTQ"].wait(e, 2 * T + j + 1)
                            if j == 0:
                                z["peNU"].wait(e, T)
                            z["acTQ"].inc(e.activation(dst[:, :, :].rearrange("p c k -> p (c k)"), bank[4 + j][:, :], ACT.Copy))

                def sc(T, u):
                    if pe:
                        z["acTQ"].wait(e, 2 * T + 2)
                        z["dvAT"].wait(e, 4 * T)
                        for c in range(4):
                            for r in range(4):
                                rg = slice(32 * r, 32 * r + 32)
                                i = e.matmul(bank[4 + r][:, c * P:(c + 1) * P], kT0[rg, c, :], qT0[rg, c, :],
                                             start=True, stop=True)
                        z["peAT"].inc(i)
                    if dv:
                        z["peAT"].wait(e, T + 1)
                        z["peNU"].wait(e, T)
                        for r in range(4):
                            z["dvAT"].inc(e.tensor_tensor(
                                at[r][:, :, :], bank[4 + r][:, :].rearrange("p (c k) -> p c k", c=4),
                                causal.unsqueeze(1).to_broadcast([P, 4, P]), ALU.mult))

                def delta(T, u):
                    r = u % 2
                    if pe:
                        z["acV"].wait(e, T + 1)
                        z["dvQK"].wait(e, T + 1)
                        z["acTY"].wait(e, T)
                        z["acHT"].wait(e, T + 2 if last_h(T) else T + 1)
                        for c in range(4):
                            i = e.matmul(bank[0][:, c * 4 * VA:(c + 1) * 4 * VA],
                                         qkp[r][:, 1, 4 * c:4 * c + 4, :].rearrange("p h d -> p (h d)"),
                                         va[r][:, 4 * c:4 * c + 4, :].rearrange("p h d -> p (h d)"), start=True, stop=True)
                        z["peDL"].inc(i)
                    if dv:
                        z["peDL"].wait(e, T + 1)
                        z["dvSB"].wait(e, T)
                        keep = misc[:, bass.ds(T + MK, 1)]
                        z["dvDL"].inc(e.scalar_tensor_tensor(
                            dl[:, :, :], bank[0][:, 0:4 * 4 * VA].rearrange("p (c x) -> p c x", c=4), keep,
                            blk.unsqueeze(1).to_broadcast([P, 4, 4 * VA]), ALU.mult, ALU.mult))

                def last_h(T):
                    return not (isinstance(T, int) and T == NT - 1)

                def num(T, u):
                    r2 = u % 2
                    if pe:
                        z["dvSB"].wait(e, T)
                        z["dvAT"].wait(e, 4 * T + 4)
                        z["acV"].wait(e, T + 1)
                        z["dvY"].wait(e, T)
                        for c in range(4):
                            e.matmul(bank[3][:, c * 4 * VA:(c + 1) * 4 * VA], qT0[:, c, :], Sbd[:, c, :],
                                     start=(c == 0), stop=False, skip_group_check=True)
                        for h in range(H0):
                            i = e.matmul(bank[3][:, h * VA:(h + 1) * VA], at[h % 4][:, h // 4, :], va[r2][:, h, :],
                                         start=False, stop=(h == H0 - 1), skip_group_check=True)
                        z["peNU"].inc(i)
                    if dv:
                        z["peNU"].wait(e, T + 1)
                        z["dvDL"].wait(e, T + 1)
                        keep = misc[:, bass.ds(T + MK, 1)]
                        z["dvSB"].inc(e.scalar_tensor_tensor(flat(Sbd[:, :, :]), flat(Sbd[:, :, :]), keep, flat(dl[:, :, :]),
                                                             ALU.mult, ALU.add))
                        v = bank[3][:, 0:H0 * VA].rearrange("p (h d) -> p h d", h=H0)
                        z["dvDN"].inc(e.tensor_scalar(dn[:, :], v[:, :, D0], 1e-6, None, ALU.add))
                        z["dvDN"].wait(e, T + 1)
                        z["dvRC"].inc(e.reciprocal(rc[:, :], dn[:, :]))
                        z["dvRC"].wait(e, T + 1)
                        z["peTY"].wait(e, T)
                        z["dvY"].inc(e.tensor_tensor(y0[:, :].rearrange("p (h d) -> p h d", h=H0), v[:, :, 0:D0],
                                                     rc[:, :].unsqueeze(2).to_broadcast([P, H0, D0]), ALU.mult))

                def ty(T, u):
                    if pe:
                        z["dvY"].wait(e, T + 1)
                        z["acHT"].wait(e, T + 3 if not (isinstance(T, int) and T > NT - 3) else NT)
                        for k in range(KD):
                            i = e.transpose(bank[0][:, k * P:(k + 1) * P], y0[:, k * P:(k + 1) * P], identf)
                        z["peTY"].inc(i)
                    if ac:
                        z["peTY"].wait(e, T + 1)
                        z["pePR"].wait(e, T)
                        z["acTY"].inc(e.activation(yT0[:, :], bank[0][:, 0:D], ACT.Copy))

                def pr(T, u, vlast):
                    if pe:
                        z["acTY"].wait(e, T + 1)
                        z["acV"].wait(e, vlast + 1)
                        for k in range(KD):
                            i = e.matmul(bank[2][:, 0:D], yT0[:, k * P:(k + 1) * P], wp[:, k, :],
                                         start=(k == 0), stop=(k == KD - 1))
                        z["pePR"].inc(i)
                    if dv:
                        z["pePR"].wait(e, T + 1)
                        z["dvX"].inc(e.tensor_tensor(tile(X, T), bank[2][:, 0:D], tile(X, T), ALU.add))

                def iteration(it, last):
                    for u in range(U):
                        T = U * it + u
                        def end(k):
                            return last and u + k >= U
                        first = isinstance(it, int) and T == 0
                        sc(T, u)
                        if not end(3):
                            ln1(T + 3, u + 3)
                        if not first:
                            ty(T - 1, u - 1)
                        if not end(1):
                            qkv(T + 1, u + 1)
                        if not first:
                            pr(T - 1, u - 1, T + 1 if not end(1) else T)
                        delta(T, u)
                        if not end(1):
                            feat(T + 1, u + 1)
                        num(T, u)
                        if not end(3):
                            ln2(T + 3, u + 3)
                        if not end(2):
                            tr(T + 2, u + 2)
                        if not end(1):
                            tq(T + 1, u + 1)

                for T in range(3):
                    ln1(T, T)
                    ln2(T, T)
                    if T < 2:
                        tr(T, T)
                qkv(0, 0)
                feat(0, 0)
                tq(0, 0)
                iteration(0, False)
                loop(NIT - 2, lambda i: iteration(i + 1, False))
                iteration(NIT - 1, True)
                ty(NT - 1, U - 1)
                pr(NT - 1, U - 1, NT - 1)
                z["dvX"].wait(e, NT)

            def loads_gate():
                def w(name):
                    return a[name].rearrange("(k p) n -> p k n", p=P)

                def row(name):
                    return a[name].rearrange("(a n) -> a n", a=1).to_broadcast([P, D])
                load(wkv[:, :, 0:D], w("L1_attn_Wk"), "raw")
                load(wkv[:, :, D:2 * D], w("L1_attn_Wv"), "raw")
                for dst, name in ((wqg, "L1_attn_Wq"), (wug, "L1_attn_Wu"), (wog, "L1_attn_Wo")):
                    load(dst, w(name), "raw")
                for dst, name in ((bkv[:, 0:D], "bk"), (bkv[:, D:2 * D], "bv"), (burow, "bu"), (lnw, "ln_w"), (lnb, "ln_b"),
                                  (borow, "bo")):
                    load(dst, row("L1_attn_" + name), "raw2")
                load(vec[:, 0:KD], a["L1_attn_bq"].rearrange("(k p) -> p k", p=P), "small", True)

            def gated_attention():
                if not sp:
                    loaded("raw")
                    loaded("raw2")
                    loaded("small")
                bd = misc[:, MD:MD + P]
                NCL = 8

                def ln1(b):
                    if dv:
                        for t in range(TB):
                            i = e.bn_stats(st1[:, t, :], tile(X, TB * b + t))
                        g["dvST"].inc(i)
                        g["dvST"].wait_alone(e, b + 1, s_passed)
                        for t in range(TB):
                            i = e.bn_aggr(mv1[:, t, :], st1[:, t, :])
                        g["dvAG"].inc(i)
                    if pl:
                        g["dvAG"].wait(e, b + 1)
                        g["plRV"].inc(e.tensor_tensor(rv1[:, :], mv1[:, :, 1], eps[:, 0:TB], ALU.add))
                        g["plRV"].wait(e, 2 * b + 1)
                        g["plRV"].inc(e.tensor_tensor(rv1[:, :], rv1[:, :], mhalf[:, 0:TB], ALU.pow))

                def ln2(b, t):
                    T = TB * b + t
                    if dv:
                        g["plRV"].wait(e, 2 * b + 2)
                        g["peTR"].wait(e, T - 1)
                        g["dvXN"].inc(e.tensor_scalar(Xn1[t % 2][:, :], tile(X, T), mv1[:, t, 0:1], rv1[:, t:t + 1],
                                                      ALU.subtract, ALU.mult))

                def tr(b, t):
                    T = TB * b + t
                    if pe:
                        g["dvXN"].wait(e, T + 1)
                        g["acHT"].wait(e, T)
                        g["acTY"].wait(e, TB * b)
                        for k in range(KD):
                            i = e.transpose(bank[0][:, k * P:(k + 1) * P], Xn1[t % 2][:, k * P:(k + 1) * P], identf)
                        g["peTR"].inc(i)
                    if ac:
                        g["peTR"].wait(e, T + 1)
                        g["acHT"].inc(e.activation(h1[:, :, t * P:(t + 1) * P],
                                                   bank[0][:, 0:D].rearrange("p (k x) -> p k x", k=KD), ACT.Copy))

                def kv(b, t):
                    T = TB * b + t
                    o = bank[1 + t % 2]
                    if pe:
                        g["acHT"].wait(e, T + 1)
                        g["dvKV"].wait(e, T - 1)
                        g["dvX"].wait(e, TB * b)
                        for k in range(KD):
                            i = e.matmul(o[:, :], h1[:, k, t * P:(t + 1) * P], wkv[:, k, :], start=(k == 0), stop=(k == KD - 1))
                        g["peKV"].inc(i)
                    if dv:
                        g["peKV"].wait(e, T + 1)
                        g["peKK"].wait(e, T - 1)
                        g["dvKV"].inc(e.tensor_tensor(kvb[t % 2][:, :], o[:, :], bkv, ALU.add))
                    if ac:
                        g["dvKV"].wait(e, T + 1)
                        g["peKK"].wait(e, T - 1)
                        g["acK"].inc(e.activation(kb[t % 2][:, :], kvb[t % 2][:, 0:D], ACT.Relu))

                def kk(b, t):
                    T = TB * b + t
                    if pe:
                        g["acK"].wait(e, T + 1)
                        if t == 0:
                            g["dvC"].wait(e, NCL * b)
                        for x in range(KD):
                            c = slice(x * P, (x + 1) * P)
                            i = e.matmul(bank[3][:, c], kb[t % 2][:, c], kvb[t % 2][:, D + x * P:D + (x + 1) * P],
                                         start=(t == 0 and x == 0), stop=(t == TB - 1 and x == KD - 1), skip_group_check=True)
                        g["peKK"].inc(i)

                def clamp(b):
                    if dv:
                        n = [NCL * b]
                        kv_ = bank[3][:, 0:D]

                        def do(i):
                            g["dvC"].inc(i)
                            n[0] = n[0] + 1
                            g["dvC"].wait(e, n[0])
                        g["peKK"].wait(e, TB * b + TB)
                        g["peO"].wait(e, TB * b)
                        do(e.tensor_scalar(ng[:, :], kv_, -1.0, None, ALU.mult))
                        do(e.tensor_tensor(ab[:, :], kv_, ng[:, :], ALU.max))
                        do(e.tensor_scalar(ab[:, :], ab[:, :], 0.01, 100.0, ALU.max, ALU.min))
                        do(e.tensor_scalar(sg[:, :], kv_, 0.0, None, ALU.is_gt))
                        do(e.tensor_scalar(ng[:, :], kv_, 0.0, None, ALU.is_lt))
                        do(e.tensor_tensor(sg[:, :], sg[:, :], ng[:, :], ALU.subtract))
                        do(e.tensor_tensor(ab[:, :], ab[:, :], sg[:, :], ALU.mult))
                        do(e.tensor_tensor(kvm[:, :].rearrange("p (a c) -> p a c", a=KD),
                                           ab[:, :].rearrange("p (a c) -> p a c", a=KD),
                                           bd.unsqueeze(1).to_broadcast([P, KD, P]), ALU.mult))

                def q(b):
                    for i in range(4):
                        c, hf = i // 2, i % 2
                        w = slice(hf * 512, (hf + 1) * 512)
                        o = bank[4 + i % 2]
                        if pe:
                            g["acQ"].wait(e, 4 * b + i - 1)
                            g["dvU"].wait(e, TB * b)
                            for k in range(KD):
                                ins = e.matmul(o[:, :], wqg[:, k, c * P:(c + 1) * P], h1[:, k, w], start=(k == 0), stop=(k == KD - 1))
                            g["peQ"].inc(ins)
                        if ac:
                            g["peQ"].wait(e, 4 * b + i + 1)
                            g["acQ"].inc(e.activation(q1[:, c, w], o[:, :], ACT.Relu, bias=vec[:, c:c + 1]))

                def bo(b):
                    if pl:
                        g["dvXN"].wait(e, TB * b + TB)
                        v = X[:, bass.ds(TB * b, TB), :]
                        g["plBO"].inc(e.tensor_tensor(v, v, borow.unsqueeze(1).to_broadcast([P, TB, D]), ALU.add))

                def out_(b, t):
                    T = TB * b + t
                    o = bank[6 + t % 2][:, 0:D]
                    if pe:
                        g["acQ"].wait(e, 4 * b + 4)
                        g["dvC"].wait(e, NCL * b + NCL)
                        g["acO"].wait(e, T - 1)
                        for x in range(KD):
                            i = e.matmul(o[:, x * P:(x + 1) * P], q1[:, x, t * P:(t + 1) * P], kvm[:, x * P:(x + 1) * P],
                                         start=True, stop=True)
                        g["peO"].inc(i)
                    if dv:
                        g["peO"].wait(e, T + 1)
                        g["dvS2"].inc(e.bn_stats(st2[:, t, :], o))
                    if ac:
                        g["dvS2"].wait(e, T + 1)
                        g["dvO"].wait(e, TB * b)
                        g["acO"].inc(e.activation(oA[:, t, :], o, ACT.Copy))

                def ln3(b):
                    if dv:
                        g["dvS2"].wait_alone(e, TB * b + TB, s_passed)
                        for t in range(TB):
                            i = e.bn_aggr(mv2[:, t, :], st2[:, t, :])
                        g["dvA2"].inc(i)
                    if pl:
                        g["dvA2"].wait(e, b + 1)
                        g["plR2"].inc(e.tensor_tensor(rv2[:, :], mv2[:, :, 1], eps[:, 0:TB], ALU.add))
                        g["plR2"].wait(e, 2 * b + 1)
                        g["plR2"].inc(e.tensor_tensor(rv2[:, :], rv2[:, :], mhalf[:, 0:TB], ALU.pow))

                def u_(b, t):
                    T = TB * b + t
                    r = t % 2
                    o = bank[4 + r][:, 0:D]
                    if pe:
                        g["dvU"].wait(e, T - 1)
                        g["acQ"].wait(e, 4 * b + 4)
                        for k in range(KD):
                            i = e.matmul(o, h1[:, k, t * P:(t + 1) * P], wug[:, k, :], start=(k == 0), stop=(k == KD - 1))
                        g["peU"].inc(i)
                    if dv:
                        g["plR2"].wait(e, 2 * b + 2)
                        g["acO"].wait(e, TB * b + t + 1)
                        g["dvY"].wait(e, T - 1)
                        g["dvO"].inc(e.tensor_scalar(o1[r][:, :], oA[:, t, :], mv2[:, t, 0:1], rv2[:, t:t + 1],
                                                     ALU.subtract, ALU.mult))
                        g["peU"].wait(e, T + 1)
                        g["dvU"].inc(e.tensor_tensor(us[r][:, :], o, burow, ALU.add))
                    if pl:
                        g["dvO"].wait(e, T + 1)
                        g["plO"].inc(e.tensor_tensor(o1[r][:, :], o1[r][:, :], lnw, ALU.mult))
                        g["plO"].wait(e, 2 * T + 1)
                        g["plO"].inc(e.tensor_tensor(o1[r][:, :], o1[r][:, :], lnb, ALU.add))

                def y_(b, t):
                    T = TB * b + t
                    r = t % 2
                    if dv:
                        g["plO"].wait(e, 2 * T + 2)
                        g["dvU"].wait(e, T + 1)
                        g["peTY"].wait(e, T - 1)
                        g["dvY"].inc(e.tensor_tensor(y1[r][:, :], us[r][:, :], o1[r][:, :], ALU.mult))
                    if pe:
                        g["dvY"].wait(e, T + 1)
                        g["acHT"].wait(e, TB * b + TB)
                        g["acTY"].wait(e, T)
                        for k in range(KD):
                            i = e.transpose(bank[0][:, k * P:(k + 1) * P], y1[r][:, k * P:(k + 1) * P], identf)
                        g["peTY"].inc(i)
                    if ac:
                        g["peTY"].wait(e, T + 1)
                        g["pePR"].wait(e, T - 1)
                        g["acTY"].inc(e.activation(yT1[r][:, :], bank[0][:, 0:D], ACT.Copy))

                def pr(b, t):
                    T = TB * b + t
                    r = t % 2
                    o = bank[1 + r][:, 0:D]
                    if pe:
                        g["acTY"].wait(e, T + 1)
                        g["dvKV"].wait(e, TB * b + TB)
                        g["dvX"].wait(e, T - 1)
                        for k in range(KD):
                            i = e.matmul(o, yT1[r][:, k * P:(k + 1) * P], wog[:, k, :], start=(k == 0), stop=(k == KD - 1))
                        g["pePR"].inc(i)
                    if dv:
                        g["pePR"].wait(e, T + 1)
                        g["plBO"].wait(e, b + 1)
                        g["dvX"].inc(e.tensor_tensor(tile(X, T), o, tile(X, T), ALU.add))

                def batch(b, last):
                    ln2(b, 0)
                    tr(b, 0)
                    for t in range(TB):
                        if t + 1 < TB:
                            ln2(b, t + 1)
                            tr(b, t + 1)
                        kv(b, t)
                        if t > 0:
                            kk(b, t - 1)
                    kk(b, TB - 1)
                    bo(b)
                    clamp(b)
                    q(b)
                    if not last:
                        ln1(b + 1)
                    for t in range(TB):
                        out_(b, t)
                    ln3(b)
                    for t in range(TB + 2):
                        if t < TB:
                            u_(b, t)
                        if 1 <= t <= TB:
                            y_(b, t - 1)
                        if t >= 2:
                            pr(b, t - 2)

                ln1(0)
                loop(B - 1, lambda b: batch(b, False))
                batch(B - 1, True)
                g["dvX"].wait(e, NT)

            loads_A(0)
            for c in range(2):
                ln_pass(c)
                for l in range(DEPTH):
                    run = DEPTH * c + l
                    prep_A()
                    loads_B(l)
                    pass_A(run)
                    prep_B()
                    if l + 1 < DEPTH:
                        loads_A(l + 1)
                    elif c == 0:
                        loads_lin()
                    else:
                        loads_F()
                    ffn(run, CH * GRP * run, True)
                merge(c)
                if c == 0:
                    linear_attention()
                    loads_A(0)
            prep_F()
            loads_gate()
            ffn(NRUN, CH * GRP * NRUN, False)
            gated_attention()
            ffn(NRUN + 1, CH * GRP * NRUN + CF * GRP, False, True)

        @block.tensor
        def _(e):
            program("pe", e)

        @block.scalar
        def _(e):
            program("ac", e)

        @block.vector
        def _(e):
            program("dv", e)

        @block.gpsimd
        def _(e):
            program("pl", e)

        @block.sync
        def _(e):
            program("sp", e)


def kernel(**inputs):
    import numpy as _np
    import concourse.bacc as _bacc
    from concourse import mybir as _mybir
    from concourse.bass_utils import run_bass_kernel_spmd as _run

    nc = _bacc.Bacc("TRN2", target_bir_lowering=False, num_devices=1)
    arrays, args = {}, {}
    for name, v in {**inputs, **shape_constants()}.items():
        v = _np.ascontiguousarray(v)
        arrays[f"in_{name}"] = v
        args[name] = nc.dram_tensor(f"in_{name}", v.shape, _mybir.dt.from_np(v.dtype), kind="ExternalInput").ap()
    out = nc.dram_tensor("out_0", (B, N, D), F32, kind="ExternalOutput").ap()
    build(nc, args, out)
    r = _run(nc, [arrays], core_ids=[0])
    return r.results[0]["out_0"]
```

```python
from contextlib import ExitStack

import numpy as np

import concourse.bass as bass
from concourse import mybir

F32 = mybir.dt.float32
F32R = mybir.dt.float32r
BF16 = mybir.dt.bfloat16
ALU = mybir.AluOpType
ACT = mybir.ActivationFunctionType
AX = mybir.AxisListType

P = 128
B, N, D = 4, 1024, 256
TB = N // P
NT = B * TB
KD = D // P
DEPTH = 2
NRUN = 2 * DEPTH
HEADS, DH = 8, 64
INNER = HEADS * DH
KI = INNER // P
HID = D * 4 * 2 // 3
CH = -(-HID // P)
HTAIL = HID - (CH - 1) * P
TAILG = 64
U = 4
NIT = NT // U
GRP = NIT
SCALE = 8.0
BIG = -3.0e38
H0, D0 = 16, 16
VA = D0 + 1
FF = 1024
CF = FF // P
OFF = 16

PAIRS = [(0, 2), (1, 3), (4, 6), (5, 7)]
NG = len(PAIRS)

ATTN = {
    "pe": """sc0+0 pt3-1 k+2 pv2-1 sc1+0 pv3-1 sc2+0 pt0+0 v+2 pt1+0 ot-1 ht+3 qT+1 sc3+0 pv0+0 wo-1 kT+1
             pv1+0 pt2+0 q+3""",
    "dv": """norm_k+1 wo-2 q+2 sum_q+2 rs-1 sc1+0 on-1 k+2 sc2+0 sum_k+2 ot-1 qT+1 sc3+0 ht+3 kT+1 norm_q+2
             sc0+1""",
    "ac": """sc3-1 kT+0 pt2-1 pt3-1 q+2 k+2 sc0+0 sc1+0 pt0+0 v+2 ot-1 qT+1 ht+3 sc2+0 pt1+0""",
    "pl": "add_q+1 add_k+1 sum_k+1",
    "sp": "wo-2 ld+4",
}

LINEAR = {
    "pe": "sc3+0 delta+0 pr-1 qT+1 kT+1 ht+2 num+0 qk+2 sc0+1 ty+0 sc1+1 v+1 sc2+1",
    "dv": "ln1+3 ty-1 sc2+0 feat+1 sc3+0 delta+0 ln2+3 ht+2 num+0 pr-1 y_norm-2 qk+2 sc0+1 sc1+1 y_stats-1",
    "ac": "v+0 qk+1 qT+1 ht+2 kT+1 ty+0",
    "pl": "ln1+3 y_stats-1",
    "sp": "y_norm-2",
}


class Ev:

    def __init__(self, handle):
        self.h = handle

    def inc(self, ins, n=1):
        ins.then_inc(self.h, n)

    def wait(self, e, n):
        e.wait_ge(self.h, n + OFF)

    def wait_alone(self, e, n, passed):
        e.wait_ge(self.h, n + OFF)
        e.sem_inc(passed, 1)


def shape_constants():
    f = np.float32
    half = np.arange(0, DH, 2, dtype=f)
    inv = (f(1.0) / np.power(f(10000.0), half / f(DH))).astype(f)
    t = np.arange(N, dtype=f)
    fr = t[:, None] * inv[None, :]
    fr = np.concatenate([fr, fr], -1)
    base = (half + f(0.4 * DH)) / f(1.4 * DH)
    power = (t - f(N // 2)) / f(64.0)
    sc = np.power(base[None, :], power[:, None]).astype(f)
    sc = np.concatenate([sc, sc], -1)
    sign = np.concatenate([-np.ones(DH // 2, f), np.ones(DH // 2, f)])
    cos, sin = np.cos(fr).astype(f), np.sin(fr).astype(f)
    tabs = [SCALE * cos * sc, SCALE * sin * sc * sign, cos / sc, sin / sc * sign]
    rot = np.stack([a.astype(f).reshape(TB, P, DH).transpose(1, 0, 2) for a in tabs], 1)
    q, k = np.arange(P)[:, None], np.arange(P)[None, :]
    cur = np.where(k <= q, 0, BIG).astype(f)
    prv = np.where(k >= q, 0, BIG).astype(f)
    off = np.full((P, P), BIG, f)
    sel = np.stack([off if i % 2 == 0 else prv for i in range(NIT)], 1)
    masks = np.concatenate([cur, prv, cur, prv, prv, cur, prv, cur, sel.reshape(P, -1)], 1)
    causal = (q <= k).astype(f)
    keep = np.ones((P, NT), f)
    keep[:, TB - 1::TB] = 0
    bd = np.zeros((P, 4, VA), f)
    for r in range(4):
        bd[32 * r:32 * r + D0, r] = 1
    bd1 = np.kron(np.eye(P // D0, dtype=f), np.ones((D0, D0), f))
    misc = np.concatenate([np.eye(P, dtype=f), causal, bd.reshape(P, -1), bd1, keep], 1)
    return {"c_rot": np.ascontiguousarray(rot.reshape(P, -1)), "c_mask": masks, "c_misc": misc}


MI, MC, MB, MD, MK = 0, P, 2 * P, 2 * P + 4 * VA, 3 * P + 4 * VA
MISC = MK + NT


def build(nc, a, out):
    ctx = ExitStack()
    with ctx:
        scope = [ctx]

        def sb(name, shape, dt=F32):
            return scope[-1].enter_context(nc.sbuf_tensor(name, shape, dt))

        def ev(name):
            return Ev(ctx.enter_context(nc.semaphore(name)))

        ya = nc.dram_tensor("ya", (B * (N + 1), P), F32, kind="Internal").ap()
        yb = nc.dram_tensor("yb", (B * (N + 1), P), F32, kind="Internal").ap()
        x_v = a["L0_attn_x"].rearrange("b (t p) c -> p (b t) c", p=P)
        out_v = out.rearrange("b (t p) c -> p (b t) c", p=P)

        bank = [ctx.enter_context(nc.psum_tensor(f"bank{i}", [P, 512], F32)) for i in range(8)]

        X = sb("X", [P, NT, D])
        Y = sb("Y", [P, NT, D])
        raw = sb("raw", [P, 3072])
        raw2 = sb("raw2", [P, 2048])
        misc = sb("misc", [P, MISC])
        identf = misc[:, MI:MI + P]
        maskf = raw[:, 0:(4 + 4 + NIT) * P]
        maskb = sb("maskb", [P, (4 + 4 + NIT) * P], BF16)
        maskE, maskO = maskb[:, 0:512], maskb[:, 512:1024]
        masksel = maskb[:, 1024:].rearrange("p (i k) -> p i k", i=NIT)
        mask0 = sb("mask0", [P, 512], BF16)
        identb = sb("identb", [P, P], BF16)
        mhalf = sb("mhalf", [P, 16])
        eps = sb("eps", [P, TB])
        rotc = sb("rotc", [P, 4, TB, DH])
        scales = sb("scales", [P, 2 * DH])
        brow = sb("brow", [P, D])
        vec = sb("vec", [P, 32])
        bias1 = sb("bias1", [P, 2 * CH + 4])
        stats = [sb(f"stats{i}", [P, U, 6]) for i in range(2)]
        meanvar = [sb(f"meanvar{i}", [P, U, 2]) for i in range(2)]
        rstd = [sb(f"rstd{i}", [P, U]) for i in range(2)]
        st, mv, rv = stats[0], meanvar[0], rstd[0]
        HB = sb("HB", [P, U, D])
        zrow = HB[0:B, 0, 0:P]

        s_raw, s_raw2, s_small = ev("raw"), ev("raw2"), ev("small")
        s_prepA, s_prepB, s_prepV, s_prepP = ev("prepA"), ev("prepB"), ev("prepV"), ev("prepP")

        scope.append(ExitStack())
        wq_h, wq_l = sb("wqkv_hi", [P, KD, 3 * INNER], F32R), sb("wqkv_lo", [P, KD, 3 * INNER], F32R)
        wo_h, wo_l = sb("wo_hi", [P, KI, D], F32R), sb("wo_lo", [P, KI, D], F32R)
        rot = sb("rot", [P, 4, TB, DH])
        H = [sb(f"H{i}", [P, D]) for i in range(U)]
        hTh = [sb(f"hT_hi{i}", [P, D], F32R) for i in range(2)]
        hTl = [sb(f"hT_lo{i}", [P, D], F32R) for i in range(2)]
        t1 = sb("rot_t1", [P, 2 * INNER])
        t2 = sb("rot_t2", [P, 2 * INNER])
        qk = [sb(f"qk{i}", [P, 2 * INNER]) for i in range(2)]
        ss, rn = sb("ss", [P, 16]), sb("rn", [P, 16])
        qTh = [sb(f"qT_hi{i}", [P, INNER], F32R) for i in range(2)]
        qTl = [sb(f"qT_lo{i}", [P, INNER], F32R) for i in range(2)]
        kTh, kTl = sb("kT_hi", [P, KI, 2, P], F32R), sb("kT_lo", [P, KI, 2, P], F32R)
        V = [sb(f"V{i}", [P, INNER]) for i in range(U)]
        nm = [sb(f"nmax{i}", [P, HEADS]) for i in range(2)]
        sums = [sb(f"sums{i}", [P, HEADS]) for i in range(2)]
        Pb = [sb(f"prob{i}", [P, 512]) for i in range(2)]
        PTs = [sb(f"probT{i}", [P, 512]) for i in range(2)]
        rs = sb("rsum", [P, HEADS])
        On = sb("On", [P, INNER])
        OTh, OTl = sb("OT_hi", [P, INNER], F32R), sb("OT_lo", [P, INNER], F32R)
        scope.pop().close()

        scope.append(ExitStack())
        w1_h, w1_l = sb("w1_hi", [P, KD, (2 * CH - 1) * P], F32R), sb("w1_lo", [P, KD, (2 * CH - 1) * P], F32R)
        w2_h, w2_l = sb("w2_hi", [P, CF, D], F32R), sb("w2_lo", [P, CF, D], F32R)
        Xn = sb("Xn", [P, U, D])
        gTh, gTl = sb("gT_hi", [P, KD, 512], F32R), sb("gT_lo", [P, KD, 512], F32R)
        gate = [sb(f"gate{i}", [P, 512]) for i in range(2)]
        hid = [sb(f"hid{i}", [P, 512]) for i in range(2)]
        hidh, hidl = sb("hid_hi", [P, CF, 512], F32R), sb("hid_lo", [P, CF, 512], F32R)
        gF = [sb(f"gT_full{k}", [P, 512]) for k in range(KD)]
        thr = sb("thr", [P, 4])
        ones = sb("ones", [P, P])
        scope.pop().close()

        scope.append(ExitStack())
        wa = raw[:, 0:KD * 3 * D].rearrange("p (k n) -> p k n", k=KD)
        wp = raw[:, KD * 3 * D:KD * 4 * D].rearrange("p (k n) -> p k n", k=KD)
        Xn0 = [sb(f"lnx{i}", [P, D]) for i in range(2)]
        st0, mv0, rv0 = sb("st0", [P, 2, 6]), sb("mv0", [P, 2, 2]), sb("rv0", [P, 2])
        wa_h, wa_l = sb("wattn_hi", [P, KD, 3 * D], F32R), sb("wattn_lo", [P, KD, 3 * D], F32R)
        wp_h, wp_l = sb("wproj_hi", [P, KD, D], F32R), sb("wproj_lo", [P, KD, D], F32R)
        h0h = [sb(f"h0T_hi{i}", [P, D], F32R) for i in range(2)]
        h0l = [sb(f"h0T_lo{i}", [P, D], F32R) for i in range(2)]
        mn, ex = sb("qk_min", [P, 512]), sb("qk_exp", [P, 512])
        qkp = [sb(f"qk_pad{i}", [P, 2, H0, 32]) for i in range(2)]
        va = [sb(f"v_one{i}", [P, H0, VA]) for i in range(2)]
        qT0 = [sb(f"linqT{i}", [P, 4, P]) for i in range(2)]
        kT0 = [sb(f"linkT{i}", [P, 4, P]) for i in range(2)]
        at = [sb(f"at{i}", [P, 4, P]) for i in range(4)]
        Sbd = sb("state", [P, 4, 4 * VA])
        dl = sb("delta", [P, 4, 4 * VA])
        rc = sb("rden", [P, H0])
        dn = sb("den", [P, H0])
        y0 = sb("y0", [P, D])
        yTh, yTl = sb("yT0_hi", [P, D], F32R), sb("yT0_lo", [P, D], F32R)
        scope.pop().close()

        scope.append(ExitStack())
        sb("kept_ternary", [P, 2 * KD * (2 * CH - 1) * P + CF * D])
        wgate = raw[:, 0:5 * KD * D]
        wg_h, wg_l = sb("wgate_hi", [P, 5 * KD * D], F32R), sb("wgate_lo", [P, 5 * KD * D], F32R)

        def gate_weight(x, i, n=1):
            return x[:, KD * D * i:KD * D * (i + n)].rearrange("p (k n) -> p k n", k=KD)
        wkv, wqg, wug, wog = (gate_weight(raw, i, n) for i, n in ((0, 2), (2, 1), (3, 1), (4, 1)))
        wkv2, wqg2, wug2, wog2 = ((gate_weight(wg_h, i, n), gate_weight(wg_l, i, n)) for i, n in ((0, 2), (2, 1), (3, 1), (4, 1)))
        bkv = raw2[:, 0:2 * D]
        burow, lnw, lnb, borow = (raw2[:, D * i:D * (i + 1)] for i in (2, 3, 4, 5))
        Xn1 = [sb(f"lny{i}", [P, D]) for i in range(2)]
        st1, mv1, rv1 = sb("st1", [P, TB, 6]), sb("mv1", [P, TB, 2]), sb("rv1", [P, TB])
        st2, mv2, rv2 = sb("st2", [P, TB, 6]), sb("mv2", [P, TB, 2]), sb("rv2", [P, TB])
        h1h, h1l = sb("h1T_hi", [P, KD, TB * P], F32R), sb("h1T_lo", [P, KD, TB * P], F32R)
        kvb = [sb(f"kv{i}", [P, 2 * D]) for i in range(2)]
        kb = [sb(f"krelu{i}", [P, D]) for i in range(2)]
        ab, sg, ng = sb("kv_abs", [P, D]), sb("kv_sign", [P, D]), sb("kv_neg", [P, D])
        kvm = sb("kvm", [P, D])
        q1 = Y[:, TB:2 * TB, :].rearrange("p t c -> p (t c)").rearrange("p (k x) -> p k x", k=KD)
        oA = Y[:, 0:TB, :]
        us = [sb(f"u{i}", [P, D]) for i in range(2)]
        o1 = [sb(f"o1_{i}", [P, D]) for i in range(2)]
        y1 = [sb(f"y1_{i}", [P, D]) for i in range(2)]
        y1h = [sb(f"y1T_hi{i}", [P, D], F32R) for i in range(2)]
        y1l = [sb(f"y1T_lo{i}", [P, D], F32R) for i in range(2)]
        scope.pop().close()

        names = """peHT acHT dvHT peQK acSQ dvRT dvSS plAD plRN dvQN peKT acKT dvKT peV acV peS dvMX acEX pePT acPT pePV
        dvRS dvON peOT acOT dvOT peWO dvY plM0
        dvST dvAG plRV dvXN peTR acHI dvLO dvGH peG peA acU dvHD xxHH dvHL peW2 dvYB plB2 sHB
        mdvY""".split()
        s = {n: ev("s_" + n) for n in names}
        s_ld = [ev(f"s_ld{i}") for i in range(U)]
        s_st = [ev(f"s_st{i}") for i in range(U)]
        s_stb = ev("s_stb")
        s_x = [ev(f"s_x{i}") for i in range(2)]
        s_passed = ctx.enter_context(nc.semaphore("s_passed"))
        s_ln = {n: ev("s_ln" + n) for n in ("dvST", "dvAG", "plRV", "dvXN", "sST")}
        z = {n: ev("z_" + n) for n in """dvST dvAG plRV dvXN peTR acHT dvHT peQK peV dvMN acEX dvQK acV peTQ acTQ
        peAT dvAT peNU peDL dvDL dvSB dvDN dvRC dvY peTY acTY dvTY pePR dvX
        dvMG dvYS dvYA plYR dvYN""".split()}
        g = {n: ev("g_" + n) for n in """dvST dvAG plRV dvXN peTR acHT peKV dvKV acK peKK dvC peQ acQ peO dvS2 dvA2 acO
        plR2 peU dvO plO dvU dvY peTY acTY dvTY pePR dvX plBO dvHT""".split()}
        everything = ([s_raw, s_raw2, s_small, s_prepA, s_prepB, s_prepV, s_prepP, s_stb]
                      + s_x + s_ld + s_st + list(s.values()) + list(s_ln.values()) + list(z.values()) + list(g.values()))

        block = ctx.enter_context(nc.Block())

        def program(E, e):
            pe, ac, dv, pl, sp = E == "pe", E == "ac", E == "dv", E == "pl", E == "sp"
            prep = {"raw": 0, "raw2": 0, "small": 0, "A": 0, "B": 0, "V": 0, "P": 0}

            def loop(n, body):
                with e.Fori(0, n) as i:
                    body(i)

            def flat(ap):
                return ap.rearrange("p a c -> p (a c)")

            def tile(buf, T):
                return flat(buf[:, bass.ds(T, 1), :])

            def three(o, lh, ll, rh, rl, start, stop):
                e.matmul(o, lh, rh, start=start, stop=False)
                e.matmul(o, lh, rl, start=False, stop=False)
                return e.matmul(o, ll, rh, start=False, stop=stop)

            def load(dst, src, which, columns=False):
                if sp:
                    {"raw": s_raw, "raw2": s_raw2, "small": s_small}[which].inc(
                        e.dma_start(dst, src, allow_slow_non_contiguous=columns), 16)
                prep[which] += 16

            def loaded(which):
                {"raw": s_raw, "raw2": s_raw2, "small": s_small}[which].wait(e, prep[which])

            def dve(f):
                if dv:
                    s_prepV.inc(f())
                prep["V"] += 1

            def act(f):
                if ac:
                    s_prepA.inc(f())
                prep["A"] += 1

            def pool(f):
                if pl:
                    s_prepB.inc(f())
                prep["B"] += 1

            def tens(f):
                if pe:
                    s_prepP.inc(f())
                prep["P"] += 1

            def sync(who, *on):
                if who == E:
                    for x in on:
                        {"V": s_prepV, "A": s_prepA, "B": s_prepB, "P": s_prepP}[x].wait(e, prep[x])

            if sp:
                for x in everything:
                    e.sem_inc(x.h, OFF)

            load(misc[:, :], a["c_misc"], "small")
            load(maskf, a["c_mask"], "raw")
            load(rotc[:, :, :, :].rearrange("p a t d -> p (a t d)"), a["c_rot"], "small")
            if not sp:
                loaded("small")
                loaded("raw")
            dve(lambda: e.tensor_copy(maskb[:, :], maskf))
            dve(lambda: e.tensor_copy(identb[:, :], identf))
            dve(lambda: e.memset(mhalf[:, :], -0.5))
            dve(lambda: e.memset(eps[:, :], 1e-5))
            dve(lambda: e.memset(zrow, 0.0))
            for who in ("sp", "pe", "ac", "pl", "dv"):
                sync(who, "V")
            if sp:
                for y in (ya, yb):
                    s_small.inc(e.dma_start(y.rearrange("(b n) c -> b n c", b=B)[:, 0, :], zrow), 16)
            prep["small"] += 32
            if sp:
                loaded("small")

            def ln_pass():
                def stats_of(n, r):
                    if dv:
                        s_x[r].wait_alone(e, 16 * (n // 2 + 1), s_passed)
                        for u in range(U):
                            i = e.bn_stats(stats[r][:, u, :], tile(X, U * n + u))
                        s_ln["dvST"].inc(i)
                        s_ln["dvST"].wait_alone(e, n + 1, s_passed)
                        for u in range(U):
                            i = e.bn_aggr(meanvar[r][:, u, :], stats[r][:, u, :])
                        s_ln["dvAG"].inc(i)
                    if pl:
                        s_ln["dvAG"].wait(e, n + 1)
                        s_ln["plRV"].inc(e.tensor_tensor(rstd[r][:, :], meanvar[r][:, :, 1], eps[:, 0:U], ALU.add))
                        s_ln["plRV"].wait(e, 2 * n + 1)
                        s_ln["plRV"].inc(e.tensor_tensor(rstd[r][:, :], rstd[r][:, :], mhalf[:, 0:U], ALU.pow))

                def norm(n, r):
                    T = U * n
                    if dv:
                        s_ln["plRV"].wait(e, 2 * n + 2)
                        for u in range(U):
                            s_ln["dvXN"].inc(e.tensor_scalar(tile(Y, T + u), tile(X, T + u), meanvar[r][:, u, 0:1],
                                                             rstd[r][:, u:u + 1], ALU.subtract, ALU.mult))
                    if sp:
                        s_ln["dvXN"].wait(e, U * (n + 1))
                        dst = ya[bass.ds(P * T + n // 2 + 1, U * P), :].rearrange("(u p) c -> p u c", p=P)
                        s_ln["sST"].inc(e.dma_start(dst, Y[:, bass.ds(T, U), P:D]), 16)

                def two(i, last):
                    stats_of(2 * i + 1, 1)
                    norm(2 * i, 0)
                    if not last:
                        stats_of(2 * i + 2, 0)
                    norm(2 * i + 1, 1)

                if dv or pl or sp:
                    stats_of(0, 0)
                    loop(GRP // 2 - 1, lambda i: two(i, False))
                    two(GRP // 2 - 1, True)
                s_ln["dvXN"].wait(e, NT)
                if sp:
                    s_ln["sST"].wait(e, 16 * GRP)

            def loads_A(l):
                one = bass.ds(l, 1)
                load(raw[:, :].rearrange("p (k n) -> p k n", k=KD),
                     a["L0_ffn_wqkv"][one, :, :].rearrange("a (k p) n -> p (a k) n", p=P), "raw")
                load(raw2[:, 0:KI * D].rearrange("p (k n) -> p k n", k=KI),
                     a["L0_ffn_wo"][one, :, :].rearrange("a (k p) n -> p (a k) n", p=P), "raw2")
                for i, name in enumerate(("L0_ffn_q_scale", "L0_ffn_k_scale")):
                    load(scales[:, i * DH:(i + 1) * DH], a[name][one, :].to_broadcast([P, DH]), "small")

            def prep_A():
                if not sp:
                    loaded("raw")
                    loaded("raw2")
                    loaded("small")
                sections = [slice(i * INNER, (i + 1) * INNER) for i in range(3)]
                raw3 = raw[:, :].rearrange("p (k n) -> p k n", k=KD)
                for w in sections:
                    act(lambda: e.activation(wq_h[:, :, w], raw3[:, :, w], ACT.Copy))
                    sync("dv", "A")
                    dve(lambda: e.tensor_tensor(wq_l[:, :, w], raw3[:, :, w], wq_h[:, :, w].bitcast(F32), ALU.subtract))
                act(lambda: e.activation(flat(wo_h[:, :, :]), raw2[:, 0:KI * D], ACT.Copy))
                sync("dv", "A")
                dve(lambda: e.tensor_tensor(flat(wo_l[:, :, :]), raw2[:, 0:KI * D], flat(wo_h[:, :, :]).bitcast(F32), ALU.subtract))
                for j in range(2):
                    sc_ = scales[:, j * DH:(j + 1) * DH]
                    c_, s_ = rot[:, 2 * j, :, :], rot[:, 2 * j + 1, :, :]
                    c0, s0 = rotc[:, 2 * j, :, :], rotc[:, 2 * j + 1, :, :]
                    pool(lambda: e.tensor_tensor(c_, c0, sc_.unsqueeze(1).to_broadcast([P, TB, DH]), ALU.mult))
                    hf = DH // 2
                    pool(lambda: e.tensor_tensor(s_[:, :, 0:hf], s0[:, :, 0:hf],
                                                 sc_[:, hf:DH].unsqueeze(1).to_broadcast([P, TB, hf]), ALU.mult))
                    pool(lambda: e.tensor_tensor(s_[:, :, hf:DH], s0[:, :, hf:DH],
                                                 sc_[:, 0:hf].unsqueeze(1).to_broadcast([P, TB, hf]), ALU.mult))
                pool(lambda: e.memset(kTh[:, :, :, :].bitcast(F32), 0.0))
                pool(lambda: e.memset(kTl[:, :, :, :].bitcast(F32), 0.0))
                pool(lambda: e.memset(V[U - 1][:, :], 0.0))
                pool(lambda: e.tensor_copy(mask0[:, :], maskE))
                for who in ("pe", "ac", "pl", "dv", "sp"):
                    sync(who, "A", "V", "B")

            def pipeline(order, steps, extra=None, lead_in=True):
                mine = []
                for word in order[E].split():
                    cut = max(word.rfind("+"), word.rfind("-"))
                    mine.append((steps[word[:cut]], int(word[cut:])))
                lead = max([k for _, k in mine], default=0)
                lag = -min([k for _, k in mine], default=0)

                def slot(T, u, known):
                    for f, k in mine:
                        if not known or 0 <= T + k < NT:
                            f(T + k, (u + k) % U)

                def iteration(it, known):
                    for u in range(U):
                        slot(U * it + u, u, known)
                        if extra:
                            extra(it, u)

                assert lead <= U and lag <= U
                for T in range(-lead if lead_in else 0, 0):
                    slot(T, T % U, True)
                if not (mine or extra):
                    return
                iteration(0, True)
                loop(NIT - 2, lambda i: iteration(i + 1, False))
                iteration(NIT - 1, True)
                for T in range(NT, NT + lag):
                    slot(T, T % U, True)

            def by(step, i):
                return lambda T, u: step(T, u, i)

            def before(T):
                return min(T, NT - 1) if isinstance(T, int) else T

            def attn_steps(run):
                R0 = NT * run

                def ld(T, u):
                    if sp:
                        s["peHT"].wait(e, R0 + T - (U - 1))
                        row = P * T + (T // TB)
                        s_ld[u].inc(e.dma_start(H[u][:, 0:P], tile(Y, T)[:, 0:P]), 16)
                        s_ld[u].inc(e.dma_start(H[u][:, P:D], ya[bass.ds(row, P), :]), 16)

                def ht(T, u):
                    if pe:
                        s_ld[u].wait(e, 32 * ((R0 + T - u) // U + 1))
                        s["acSQ"].wait(e, 2 * (R0 + T))
                        s["dvRT"].wait(e, 4 * (R0 + T))
                        e.transpose(bank[1][:, 0:P], H[u][:, 0:P], identf)
                        s["peHT"].inc(e.transpose(bank[1][:, P:D], H[u][:, P:D], identf))
                    if ac:
                        s["peHT"].wait(e, R0 + T + 1)
                        s["acHT"].inc(e.activation(hTh[u % 2][:, :], bank[1][:, 0:D], ACT.Copy))
                    if dv:
                        s["acHT"].wait(e, R0 + T + 1)
                        s["dvHT"].inc(e.tensor_tensor(hTl[u % 2][:, :], bank[1][:, 0:D],
                                                      hTh[u % 2][:, :].bitcast(F32), ALU.subtract))

                def proj(o, u, c0, n):
                    for k in range(KD):
                        w = (slice(None), k, slice(c0, c0 + n))
                        lt = slice(k * P, (k + 1) * P)
                        i = three(o, hTh[u % 2][:, lt], hTl[u % 2][:, lt], wq_h[w], wq_l[w], k == 0, k == KD - 1)
                    return i

                def heads(x):
                    return x.rearrange("p (h d) -> p h d", h=HEADS)

                def half(u, j):
                    return qk[u % 2][:, j * INNER:(j + 1) * INNER]

                def qk_(T, u, j):
                    G = R0 + T
                    if pe:
                        s["dvHT"].wait(e, G + 1)
                        s["dvKT"].wait(e, 2 * (G - 2) + j + 1)
                        s["peQK"].inc(proj(bank[j][:, :], u, INNER * j, INNER))
                    if ac:
                        s["peQK"].wait(e, 2 * G + j + 1)
                        s["acSQ"].inc(e.activation(half(u, j), bank[j][:, :], ACT.Square))
                    if dv:
                        s["acSQ"].wait(e, 2 * G + j + 1)
                        s["plAD"].wait(e, 2 * (G - 1) + j + 1)
                        o1_, o2_ = heads(t1[:, j * INNER:(j + 1) * INNER]), heads(t2[:, j * INNER:(j + 1) * INNER])
                        x_ = heads(bank[j][:, :])
                        hf = DH // 2

                        def tab(i, lo, hi):
                            return rot_at(i, T)[:, lo:hi].unsqueeze(1).to_broadcast([P, HEADS, hi - lo])

                        s["dvRT"].inc(e.tensor_tensor(o1_, x_, tab(2 * j, 0, DH), ALU.mult))
                        e.tensor_tensor(o2_[:, :, 0:hf], x_[:, :, hf:DH], tab(2 * j + 1, 0, hf), ALU.mult)
                        s["dvRT"].inc(e.tensor_tensor(o2_[:, :, hf:DH], x_[:, :, 0:hf], tab(2 * j + 1, hf, DH), ALU.mult))

                def rot_at(i, T):
                    pos = T - TB * (T // TB)
                    if isinstance(pos, int):
                        return rot[:, i, pos, :]
                    return flat(rot[:, i, bass.ds(nc.s_assert_within(
                        pos, 0, TB - 1, skip_runtime_bounds_check_because="the remainder of a division by TB"), 1), :])

                def sum_(T, u, j):
                    G = R0 + T
                    if dv:
                        s["acSQ"].wait(e, 2 * G + j + 1)
                        s["dvSS"].inc(e.tensor_reduce(ss[:, j * HEADS:(j + 1) * HEADS], heads(half(u, j)), AX.X, ALU.add))
                        if j == 1:
                            s["dvSS"].wait(e, 3 * G + 2)
                            s["dvSS"].inc(e.tensor_scalar(ss[:, :], ss[:, :], 1e-24, None, ALU.max))
                    if pl and j == 1:
                        s["dvSS"].wait(e, 3 * G + 3)
                        s["plRN"].inc(e.tensor_tensor(rn[:, :], ss[:, :], mhalf[:, :], ALU.pow))

                def add_(T, u, j):
                    G = R0 + T
                    if pl:
                        s["dvSS"].wait(e, 3 * G + j + 1)
                        s["dvRT"].wait(e, 4 * G + 2 * j + 2)
                        w = slice(j * INNER, (j + 1) * INNER)
                        s["plAD"].inc(e.tensor_tensor(half(u, j), t1[:, w], t2[:, w], ALU.add))

                def norm_(T, u, j):
                    G = R0 + T
                    if dv:
                        s["plRN"].wait(e, G + 1)
                        s["plAD"].wait(e, 2 * G + j + 1)
                        s["dvQN"].inc(e.tensor_tensor(
                            heads(half(u, j)), heads(half(u, j)),
                            rn[:, j * HEADS:(j + 1) * HEADS].unsqueeze(2).to_broadcast([P, HEADS, DH]), ALU.mult))

                def v_(T, u):
                    G = R0 + T
                    if pe:
                        s["acSQ"].wait(e, 2 * G + 1)
                        s["dvRT"].wait(e, 4 * G + 2)
                        s["peV"].inc(proj(bank[0][:, :], u, 2 * INNER, INNER))
                    if ac:
                        s["peV"].wait(e, G + 1)
                        s["acV"].inc(e.activation(V[u][:, :], bank[0][:, :], ACT.Copy))

                def tr_(T, u, j):
                    G = R0 + T
                    r = u % 2
                    hi = qTh[r][:, :] if j == 0 else kTh[:, :, r, :]
                    lo = qTl[r][:, :] if j == 0 else kTl[:, :, r, :]
                    src = bank[j][:, :] if j == 0 else bank[j][:, :].rearrange("p (c k) -> p c k", c=KI)
                    if pe:
                        s["dvQN"].wait(e, 2 * G + j + 1)
                        if j == 0:
                            s["acV"].wait(e, R0 + before(T + 1) + 1)
                        else:
                            s["dvHT"].wait(e, R0 + before(T + 2) + 1)
                        for c in range(KI):
                            i = e.transpose(bank[j][:, c * P:(c + 1) * P], half(u, j)[:, c * P:(c + 1) * P], identf)
                        s["peKT"].inc(i)
                    if ac:
                        s["peKT"].wait(e, 2 * G + j + 1)
                        s["acKT"].inc(e.activation(hi, src, ACT.Copy))
                    if dv:
                        s["acKT"].wait(e, 2 * G + j + 1)
                        s["dvKT"].inc(e.tensor_tensor(lo, src, hi.bitcast(F32), ALU.subtract))

                def sc_(T, u, gi):
                    G = R0 + T
                    r = u % 2
                    n = NG * G + gi
                    bk = bank[2 + gi % 2]
                    hs = PAIRS[gi]
                    if pe:
                        s["dvKT"].wait(e, 2 * G + 2)
                        s["acEX"].wait(e, n - 1)
                        if u == 0:
                            s["plM0"].wait(e, GRP * run + T // U + 1)
                        m = mask0[:, :] if u == 0 else (maskE if r == 0 else maskO)
                        e.matmul(bk[:, :], identb[:, :], m, start=True, stop=False, skip_group_check=True)
                        for i, h in enumerate(hs):
                            pp = slice(DH * (h % 2), DH * (h % 2) + DH)
                            c = h // 2
                            o, lt = bk[:, i * 256:(i + 1) * 256], slice(c * P, (c + 1) * P)
                            kh, kl = (x[pp, c, :, :].rearrange("p a k -> p (a k)") for x in (kTh, kTl))
                            e.matmul(o, qTh[r][pp, lt], kh, start=False, stop=False, skip_group_check=True)
                            e.matmul(o, qTh[r][pp, lt], kl, start=False, stop=False, skip_group_check=True)
                            ins = e.matmul(o, qTl[r][pp, lt], kh, start=False, stop=True, skip_group_check=True)
                        s["peS"].inc(ins)
                    if dv:
                        s["peS"].wait(e, n + 1)
                        s["dvMX"].inc(e.tensor_reduce(nm[r][:, 2 * gi:2 * gi + 2],
                                                      bk[:, :].rearrange("p (h k) -> p h k", h=2), AX.X, ALU.max, negate=True))
                    if ac:
                        s["dvMX"].wait(e, n + 1)
                        s["pePT"].wait(e, n - 1)
                        for i, h in enumerate(hs):
                            ins = e.activation(Pb[gi % 2][:, i * 256:(i + 1) * 256], bk[:, i * 256:(i + 1) * 256], ACT.Exp,
                                               bias=nm[r][:, 2 * gi + i:2 * gi + i + 1], accum_out=sums[r][:, h:h + 1])
                        s["acEX"].inc(ins)

                def pt_(T, u, gi):
                    n = NG * (R0 + T) + gi
                    b_ = bank[4 + gi % 2]
                    if pe:
                        s["acEX"].wait(e, n + 1)
                        s["acPT"].wait(e, n - 1)
                        for x in range(4):
                            i = e.transpose(b_[:, x * P:(x + 1) * P], Pb[gi % 2][:, x * P:(x + 1) * P], identf)
                        s["pePT"].inc(i)
                    if ac:
                        s["pePT"].wait(e, n + 1)
                        s["pePV"].wait(e, n - 1)
                        s["acPT"].inc(e.activation(PTs[gi % 2][:, :], b_[:, :], ACT.Copy))

                def pv_(T, u, gi):
                    G = R0 + T
                    n = NG * G + gi
                    if pe:
                        s["acPT"].wait(e, n + 1)
                        if gi == 0:
                            s["acV"].wait(e, G + 1)
                            s["dvON"].wait(e, G)
                        for i, h in enumerate(PAIRS[gi]):
                            for kt in range(2):
                                vt = V[u] if u % 2 == kt else V[(u - 1) % U]
                                ins = e.matmul(bank[6][:, h * DH:(h + 1) * DH],
                                               PTs[gi % 2][:, (2 * i + kt) * P:(2 * i + kt + 1) * P],
                                               vt[:, h * DH:(h + 1) * DH], start=(kt == 0), stop=(kt == 1))
                        s["pePV"].inc(ins)

                def rs_(T, u):
                    if dv:
                        s["acEX"].wait(e, NG * (R0 + T) + NG)
                        s["dvRS"].inc(e.reciprocal(rs[:, :], sums[u % 2][:, :]))

                def on_(T, u):
                    G = R0 + T
                    if dv:
                        s["dvRS"].wait(e, G + 1)
                        s["pePV"].wait(e, NG * G + NG)
                        s["peOT"].wait(e, G)
                        s["dvON"].inc(e.tensor_tensor(heads(On[:, :]), heads(bank[6][:, :]),
                                                      rs[:, :].unsqueeze(2).to_broadcast([P, HEADS, DH]), ALU.mult))

                def ot_(T, u):
                    G = R0 + T
                    if pe:
                        s["dvON"].wait(e, G + 1)
                        s["dvY"].wait(e, G)
                        for c in range(KI):
                            i = e.transpose(bank[7][:, c * P:(c + 1) * P], On[:, c * P:(c + 1) * P], identf)
                        s["peOT"].inc(i)
                    if ac:
                        s["peOT"].wait(e, G + 1)
                        s["acOT"].inc(e.activation(OTh[:, :], bank[7][:, :], ACT.Copy))
                    if dv:
                        s["acOT"].wait(e, G + 1)
                        s["dvOT"].inc(e.tensor_tensor(OTl[:, :], bank[7][:, :], OTh[:, :].bitcast(F32), ALU.subtract))

                def wo_(T, u):
                    G = R0 + T
                    if pe:
                        s["dvOT"].wait(e, G + 1)
                        for c in range(KI):
                            lt = slice(c * P, (c + 1) * P)
                            i = three(bank[7][:, 0:D], OTh[:, lt], OTl[:, lt], wo_h[:, c, :], wo_l[:, c, :], c == 0, c == KI - 1)
                        s["peWO"].inc(i)
                    if dv:
                        s["peWO"].wait(e, G + 1)
                        s["dvY"].inc(e.tensor_tensor(tile(Y, T), bank[7][:, 0:D], tile(Y, T), ALU.add))
                    if sp:
                        s["dvY"].wait(e, G + 1)
                        row = P * T + (T // TB) + 1
                        s_st[u].inc(e.dma_start(yb[bass.ds(row, P), :], tile(Y, T)[:, P:D]), 16)

                f = {"ld": ld, "ht": ht, "v": v_, "rs": rs_, "on": on_, "ot": ot_, "wo": wo_}
                for j, name in enumerate("qk"):
                    f.update({name: by(qk_, j), "sum_" + name: by(sum_, j), "add_" + name: by(add_, j),
                              "norm_" + name: by(norm_, j), name + "T": by(tr_, j)})
                for gi in range(NG):
                    f.update({f"sc{gi}": by(sc_, gi), f"pt{gi}": by(pt_, gi), f"pv{gi}": by(pv_, gi)})
                return f

            def first_tiles(run):
                if sp:
                    for T in range(U):
                        attn_steps(run)["ld"](T, T)

            def ffn_load(pas, n):
                if sp:
                    s["dvXN"].wait(e, U * (GRP * pas + n))
                    T = U * n
                    s["sHB"].inc(e.dma_start(HB[:, :, 0:P], Y[:, bass.ds(T, U), 0:P]), 16)
                    src = yb[bass.ds(P * T + n // 2, U * P), :].rearrange("(u p) c -> p u c", p=P)
                    s["sHB"].inc(e.dma_start(HB[:, :, P:D], src), 16)

            def ffn_source(l0, n, u):
                return HB[:, u, :] if l0 else tile(X, U * n + u)

            def ffn_stats(pas, l0, n):
                G = GRP * pas + n
                if dv:
                    if l0:
                        s["sHB"].wait(e, 32 * (G + 1))
                    for u in range(U):
                        i = e.bn_stats(st[:, u, :], ffn_source(l0, n, u))
                    s["dvST"].inc(i)
                    s["dvST"].wait_alone(e, G + 1, s_passed)
                    for u in range(U):
                        i = e.bn_aggr(mv[:, u, :], st[:, u, :])
                    s["dvAG"].inc(i)
                if pl:
                    s["dvAG"].wait(e, G + 1)
                    s["plRV"].inc(e.tensor_tensor(rv[:, :], mv[:, :, 1], eps[:, 0:U], ALU.add))
                    s["plRV"].wait(e, 2 * G + 1)
                    s["plRV"].inc(e.tensor_tensor(rv[:, :], rv[:, :], mhalf[:, 0:U], ALU.pow))

            def pass_A(run):
                def mask_of(it):
                    s["peS"].wait(e, NG * (NT * run + U * it - U) + NG)
                    for x in range(2):
                        i = e.tensor_copy(mask0[:, 256 * x + P:256 * x + 2 * P],
                                          masksel[:, bass.ds(it, 1), :].rearrange("p a k -> p (a k)"))
                    s["plM0"].inc(i)

                def extra(it, u):
                    last = isinstance(it, int) and it == NIT - 1
                    if pl and u == 1 and not last:
                        mask_of(it + 1)
                    if last and u == 1 and sp:
                        for x in s_st:
                            x.wait(e, 16 * (GRP * run + 1))
                        ffn_load(run, 0)
                    if last and u == U - 1:
                        ffn_stats(run, True, 0)

                if pl:
                    mask_of(0)
                pipeline(ATTN, attn_steps(run), extra, lead_in=not sp)
                s["dvY"].wait(e, NT * (run + 1))
                if sp:
                    for x in s_st:
                        x.wait(e, 16 * GRP * (run + 1))

            def loads_B(l):
                one = bass.ds(l, 1)
                W1 = raw[:, 0:KD * 2 * HID].rearrange("p (k n) -> p k n", k=KD)
                load(W1, a["L0_ffn_w1"][one, :, :].rearrange("a (k p) n -> p (a k) n", p=P), "raw")
                W2 = raw2[:, 0:CH * D].rearrange("p (k n) -> p k n", k=CH)
                load(W2[:, 0:CH - 1, :], a["L0_ffn_w2"][one, 0:(CH - 1) * P, :].rearrange("a (k p) n -> p (a k) n", p=P), "raw2")
                load(W2[0:HTAIL, CH - 1, :], a["L0_ffn_w2"][one, (CH - 1) * P:HID, :].rearrange("a p n -> (a p) n"), "raw2")
                load(vec[:, 0:KD], a["L0_ffn_ln_g"][one, :].rearrange("a (k p) -> p (a k)", p=P), "small", True)
                load(vec[:, 4:4 + KD], a["L0_ffn_ln_b"][one, :].rearrange("a (k p) -> p (a k)", p=P), "small", True)
                b1 = a["L0_ffn_b1"]
                for j in range(2):
                    load(bias1[:, j * CH:j * CH + CH - 1],
                         b1[one, j * HID:j * HID + (CH - 1) * P].rearrange("a (k p) -> p (a k)", p=P), "small", True)
                    r0 = TAILG * j
                    load(bias1[r0:r0 + HTAIL, j * CH + CH - 1:j * CH + CH],
                         b1[one, j * HID + (CH - 1) * P:(j + 1) * HID].rearrange("a p -> p a"), "small", True)
                load(brow[:, :], a["L0_ffn_b2"][one, :].to_broadcast([P, D]), "small")

            def prep_w1():
                W1 = raw[:, 0:KD * 2 * HID].rearrange("p (k n) -> p k n", k=KD)
                if not sp:
                    loaded("raw")
                    loaded("small")
                main = (CH - 1) * P
                pieces = [(main, HID, main), (0, 0, main), (2 * main, main, HTAIL), (2 * main + TAILG, HID + main, HTAIL)]
                dve(lambda: e.memset(w1_h[:, :, 2 * main:].bitcast(F32), 0.0))
                dve(lambda: e.memset(w1_l[:, :, 2 * main:].bitcast(F32), 0.0))
                for i, (d0, s0, n) in enumerate(pieces):
                    if i == 2:
                        sync("ac", "V")
                    act(lambda: e.activation(w1_h[:, :, d0:d0 + n], W1[:, :, s0:s0 + n], ACT.Copy))
                    sync("dv", "A", "V")
                    dve(lambda: e.tensor_tensor(w1_l[:, :, d0:d0 + n], W1[:, :, s0:s0 + n],
                                                w1_h[:, :, d0:d0 + n].bitcast(F32), ALU.subtract))

            def prep_w2():
                W2 = raw2[:, 0:CH * D].rearrange("p (k n) -> p k n", k=CH)
                if not sp:
                    loaded("raw2")
                for rows, c in ((slice(0, P), slice(0, CH - 1)), (slice(0, HTAIL), slice(CH - 1, CH))):
                    act(lambda: e.activation(w2_h[rows, c, :], W2[rows, c, :], ACT.Copy))
                    sync("dv", "A")
                    dve(lambda: e.tensor_tensor(w2_l[rows, c, :], W2[rows, c, :], w2_h[rows, c, :].bitcast(F32), ALU.subtract))

            def ternary(W):
                dve(lambda: e.tensor_reduce(thr[:, 0:1], W, AX.X, ALU.add, apply_absolute_value=True))
                sync("pe", "V")
                tens(lambda: e.matmul(bank[0][:, 0:1], ones[:, :], thr[:, 0:1], start=True, stop=True))
                sync("dv", "P")
                dve(lambda: e.tensor_scalar(thr[:, 1:2], bank[0][:, 0:1], 1.0 / (FF * D), 1e-5, ALU.mult, ALU.add))
                sync("dv", "V")
                dve(lambda: e.tensor_scalar(thr[:, 2:3], thr[:, 1:2], 0.5, None, ALU.mult))
                dve(lambda: e.tensor_scalar(thr[:, 3:4], thr[:, 1:2], -0.5, None, ALU.mult))
                sync("dv", "V")
                neg = Y[:, 0:TB, :].rearrange("p t c -> p (t c)")
                dve(lambda: e.tensor_scalar(neg, W, thr[:, 3:4], None, ALU.is_lt))
                dve(lambda: e.tensor_scalar(W, W, thr[:, 2:3], None, ALU.is_gt))
                sync("dv", "V")
                dve(lambda: e.tensor_tensor(W, W, neg, ALU.subtract))

            def loads_F():
                load(raw[:, 0:CF * D].rearrange("p (c n) -> p c n", c=CF), a["L1_ffn_W1"].rearrange("(c p) n -> p c n", p=P), "raw")
                load(raw2[:, :].rearrange("p (c n) -> p c n", c=KD), a["L1_ffn_W2"].rearrange("(c p) n -> p c n", p=P), "raw2")

            def prep_F():
                Wa, Wb = raw[:, 0:CF * D], raw2[:, 0:2048]
                load(bias1[:, 0:CF], a["L1_ffn_b1"].rearrange("(c p) -> p c", p=P), "small", True)
                load(brow[:, :], a["L1_ffn_b2"].rearrange("(a n) -> a n", a=1).to_broadcast([P, D]), "small")
                if not sp:
                    loaded("raw")
                    loaded("raw2")
                    loaded("small")
                dve(lambda: e.memset(ones[:, :], 1.0))
                ternary(Wa)
                ternary(Wb)
                sync("pe", "V")
                for c in range(CF):
                    for k in range(KD):
                        tens(lambda: e.transpose(bank[c // 2][:, (2 * (c % 2) + k) * P:(2 * (c % 2) + k + 1) * P],
                                                 Wa[:, c * D + k * P:c * D + (k + 1) * P], identf))
                for k in range(KD):
                    for c in range(CF):
                        tens(lambda: e.transpose(bank[4 + c // 2][:, (2 * (c % 2) + k) * P:(2 * (c % 2) + k + 1) * P],
                                                 Wb[:, k * FF + c * P:k * FF + (c + 1) * P], identf))
                sync("dv", "P")
                for c in range(CF):
                    src = bank[c // 2][:, 2 * (c % 2) * P:2 * (c % 2) * P + D]
                    dve(lambda: e.tensor_copy(w1_h[:, :, c * P:(c + 1) * P], src.rearrange("p (k f) -> p k f", k=KD)))
                    src2 = bank[4 + c // 2][:, 2 * (c % 2) * P:2 * (c % 2) * P + D]
                    dve(lambda: e.tensor_copy(w2_h[:, c, :], src2))
                dve(lambda: e.tensor_scalar(brow[:, :], brow[:, :], 0.5, None, ALU.mult))
                for who in ("pe", "ac", "pl", "dv", "sp"):
                    sync(who, "A", "V", "P")

            def ffn(pas, cb, l0, final=False, next_loads=None):
                nch = CH if l0 else CF
                G0 = GRP * pas
                R = Y if l0 else X

                def hb(n):
                    s["sHB"].wait(e, 32 * (G0 + n + 1))

                def ln2(n):
                    G = G0 + n
                    if dv:
                        s["plRV"].wait(e, 2 * G + 2)
                        s["peTR"].wait(e, 2 * G)
                        for u in range(U):
                            s["dvXN"].inc(e.tensor_scalar(Xn[:, u, :], ffn_source(l0, n, u), mv[:, u, 0:1], rv[:, u:u + 1],
                                                          ALU.subtract, ALU.mult))
                    if pl:
                        if l0:
                            hb(n)
                        else:
                            s["dvXN"].wait(e, U * G + U)
                        v = R[:, bass.ds(U * n, U), :]
                        s["plB2"].inc(e.tensor_tensor(v, v, brow[:, :].unsqueeze(1).to_broadcast([P, U, D]), ALU.add))

                def tr(n):
                    G = G0 + n
                    if pe:
                        s["dvXN"].wait(e, U * G + U)
                        s["dvLO"].wait(e, 2 * G)
                        for k in range(KD):
                            for u in range(U):
                                i = e.transpose(bank[k][:, u * P:(u + 1) * P], Xn[:, u, k * P:(k + 1) * P], identf)
                            s["peTR"].inc(i)
                    for k in range(KD):
                        if ac:
                            s["peTR"].wait(e, 2 * G + k + 1)
                            if l0:
                                s["acHI"].inc(e.activation(gF[k][:, :], bank[k][:, :], ACT.Identity,
                                                           bias=vec[:, 4 + k:5 + k], scale=vec[:, k:k + 1]))
                            else:
                                s["acHI"].inc(e.activation(gTh[:, k, :], bank[k][:, :], ACT.Copy))
                        if dv:
                            s["acHI"].wait(e, 2 * G + k + 1)
                            full = bank[k]
                            if l0:
                                full = gF[k]
                                s["dvGH"].inc(e.tensor_copy(gTh[:, k, :], full[:, :]))
                                s["dvGH"].wait(e, 2 * G + k + 1)
                            s["dvLO"].inc(e.tensor_tensor(gTl[:, k, :], full[:, :], gTh[:, k, :].bitcast(F32), ALU.subtract))

                def w1mm(o, col):
                    for k in range(KD):
                        w = (slice(None), k, slice(col, col + P))
                        if l0:
                            i = three(o, w1_h[w], w1_l[w], gTh[:, k, :], gTl[:, k, :], k == 0, k == KD - 1)
                        else:
                            e.matmul(o, w1_h[w], gTh[:, k, :], start=(k == 0), stop=False)
                            i = e.matmul(o, w1_h[w], gTl[:, k, :], start=False, stop=(k == KD - 1))
                    return i

                def piece(n, c):
                    ci = cb + nch * n + c
                    G = G0 + n
                    bg, ba = bank[2 + 2 * (c % 2)], bank[3 + 2 * (c % 2)]
                    p2 = c % 2
                    tail = l0 and c == CH - 1
                    m = HTAIL if tail else P
                    gp = slice(TAILG, TAILG + HTAIL) if tail else slice(0, P)
                    if pe:
                        if c == 0:
                            s["dvLO"].wait(e, 2 * G + 2)
                        s["dvHD" if l0 else "acU"].wait(e, ci - 1)
                        if l0:
                            s["peG"].inc(w1mm(bg[:, :], (CH - 1) * P + c * P))
                            if not tail:
                                s["peA"].inc(w1mm(ba[:, :], c * P))
                        else:
                            s["peG"].inc(w1mm(bg[:, :], c * P))
                    if l0:
                        if ac:
                            s["peG"].wait(e, ci + 1)
                            s["dvHD"].wait(e, ci - 1)
                            s["acU"].inc(e.activation(gate[p2][0:m, :], bg[gp, :], ACT.Gelu, bias=bias1[gp, CH + c:CH + c + 1]))
                        if dv:
                            s["acU"].wait(e, ci + 1)
                            if not tail:
                                s["peA"].wait(e, (CH - 1) * G + c + 1)
                            s["dvHD"].inc(e.scalar_tensor_tensor(hid[p2][0:m, :], (bg if tail else ba)[0:m, :],
                                                                 bias1[0:m, c:c + 1], gate[p2][0:m, :], ALU.add, ALU.mult))
                            s["dvHD"].wait(e, ci + 1)
                            s["peW2"].wait(e, U * G)
                            s["xxHH"].inc(e.tensor_copy(hidh[0:m, c, :], hid[p2][0:m, :]))
                    else:
                        if ac:
                            s["peG"].wait(e, ci + 1)
                            s["dvHL"].wait(e, ci - 1)
                            s["acU"].inc(e.activation(hid[p2][:, :], bg[:, :], ACT.Relu, bias=bias1[:, c:c + 1]))
                            s["acU"].wait(e, ci + 1)
                            s["peW2"].wait(e, U * G)
                            s["xxHH"].inc(e.activation(hidh[:, c, :], hid[p2][:, :], ACT.Copy))
                    if dv:
                        s["xxHH"].wait(e, ci + 1)
                        if not l0:
                            s["peW2"].wait(e, U * G)
                        s["dvHL"].inc(e.tensor_tensor(hidl[0:m, c, :], hid[p2][0:m, :], hidh[0:m, c, :].bitcast(F32), ALU.subtract))

                def w2_(n):
                    G = G0 + n
                    for u in range(U):
                        i_ = U * G + u
                        o = bank[6 + u % 2][:, 0:D]
                        if pe:
                            s["dvYB"].wait(e, i_ - 1)
                            for c in range(nch):
                                m = HTAIL if (l0 and c == CH - 1) else P
                                if u == 0:
                                    s["dvHL"].wait(e, cb + nch * n + c + 1)
                                lt = slice(u * P, (u + 1) * P)
                                if l0:
                                    i = three(o, hidh[0:m, c, lt], hidl[0:m, c, lt], w2_h[0:m, c, :], w2_l[0:m, c, :],
                                              c == 0, c == nch - 1)
                                else:
                                    e.matmul(o, hidh[:, c, lt], w2_h[:, c, :], start=(c == 0), stop=False)
                                    i = e.matmul(o, hidl[:, c, lt], w2_h[:, c, :], start=False, stop=(c == nch - 1))
                            s["peW2"].inc(i)
                        if dv:
                            s["peW2"].wait(e, i_ + 1)
                            if u == 0:
                                s["plB2"].wait(e, G + 1)
                            v = tile(R, U * n + u)
                            if l0:
                                s["dvYB"].inc(e.tensor_tensor(v, o, v, ALU.add))
                            else:
                                s["dvYB"].inc(e.scalar_tensor_tensor(v, o, 0.5, v, ALU.mult, ALU.add))
                    if sp and (l0 or final):
                        s["dvYB"].wait(e, U * G + U)
                        T = U * n
                        if l0:
                            dst = ya[bass.ds(P * T + n // 2 + 1, U * P), :].rearrange("(u p) c -> p u c", p=P)
                            s_stb.inc(e.dma_start(dst, Y[:, bass.ds(T, U), P:D]), 16)
                        else:
                            s_stb.inc(e.dma_start(out_v[:, bass.ds(T, U), :], X[:, bass.ds(T, U), :]), 16)

                def group(n, last):
                    if l0 and not last:
                        ffn_load(pas, n + 1)
                    for c in range(nch):
                        piece(n, c)
                        if c == 1 and not last:
                            ffn_stats(pas, l0, n + 1)
                        if c == 3 and not last:
                            ln2(n + 1)
                    if not last:
                        tr(n + 1)
                    w2_(n)

                if not l0:
                    ffn_stats(pas, l0, 0)
                ln2(0)
                if l0:
                    prep_w1()
                tr(0)
                if l0:
                    prep_w2()
                    for who in ("pe", "ac", "dv", "sp"):
                        sync(who, "A", "V")
                    next_loads()
                group(0, False)
                loop(GRP - 2, lambda i: group(i + 1, False))
                group(GRP - 1, True)
                s["dvYB"].wait(e, U * (G0 + GRP))
                if (sp or dv) and l0:
                    s_stb.wait(e, 16 * (G0 + GRP))
                if sp and final:
                    s_stb.wait(e, 16 * GRP * (NRUN + 1))

            def merge():
                if dv:
                    def body(n):
                        v, w = X[:, bass.ds(U * n, U), :], Y[:, bass.ds(U * n, U), :]
                        s["mdvY"].inc(e.scalar_tensor_tensor(flat(v), flat(w), 0.5, flat(v), ALU.mult, ALU.add))
                    loop(GRP, body)
                s["mdvY"].wait(e, GRP)

            def loads_lin():
                load(wa, a["L0_attn_w_attn"].rearrange("(k p) n -> p k n", p=P), "raw")
                load(wp, a["L0_attn_w_proj"].rearrange("(k p) n -> p k n", p=P), "raw")

            def linear_attention():
                if not sp:
                    loaded("raw")
                act(lambda: e.activation(flat(wa_h[:, :, :]), flat(wa), ACT.Copy))
                act(lambda: e.activation(flat(wp_h[:, :, :]), flat(wp), ACT.Copy))
                for i in range(2):
                    pool(lambda: e.memset(qkp[i][:, :, :, :], 0.0))
                    pool(lambda: e.memset(va[i][:, :, :], 1.0))
                pool(lambda: e.memset(Sbd[:, :, :], 0.0))
                sync("dv", "A")
                dve(lambda: e.tensor_tensor(flat(wa_l[:, :, :]), flat(wa), flat(wa_h[:, :, :]).bitcast(F32), ALU.subtract))
                dve(lambda: e.tensor_tensor(flat(wp_l[:, :, :]), flat(wp), flat(wp_h[:, :, :]).bitcast(F32), ALU.subtract))
                for who in ("pe", "ac", "dv", "sp"):
                    sync(who, "B", "V", "A")
                loads_A(0)
                causal = misc[:, MC:MC + P]
                blk = misc[:, MB:MB + 4 * VA]

                def ln1(T, u):
                    r = u % 2
                    if dv:
                        z["dvMG"].inc(e.scalar_tensor_tensor(tile(X, T), tile(Y, T), 0.5, tile(X, T), ALU.mult, ALU.add))
                        z["dvMG"].wait_alone(e, T + 1, s_passed)
                        z["dvST"].inc(e.bn_stats(st0[:, r, :], tile(X, T)))
                        z["dvST"].wait_alone(e, T + 1, s_passed)
                        z["dvAG"].inc(e.bn_aggr(mv0[:, r, :], st0[:, r, :]))
                    if pl:
                        z["dvAG"].wait(e, T + 1)
                        z["plRV"].inc(e.tensor_tensor(rv0[:, r:r + 1], mv0[:, r, 1:2], eps[:, 0:1], ALU.add))
                        z["plRV"].wait(e, 2 * T + 1)
                        z["plRV"].inc(e.tensor_tensor(rv0[:, r:r + 1], rv0[:, r:r + 1], mhalf[:, 0:1], ALU.pow))

                def ln2(T, u):
                    r = u % 2
                    if dv:
                        z["plRV"].wait(e, 2 * T + 2)
                        z["peTR"].wait(e, T - 1)
                        z["dvXN"].inc(e.tensor_scalar(Xn0[r][:, :], tile(X, T), mv0[:, r, 0:1], rv0[:, r:r + 1],
                                                      ALU.subtract, ALU.mult))

                def ht(T, u):
                    r = u % 2
                    if pe:
                        z["dvXN"].wait(e, T + 1)
                        z["dvDL"].wait(e, T - 1)
                        for k in range(KD):
                            i = e.transpose(bank[0][:, k * P:(k + 1) * P], Xn0[r][:, k * P:(k + 1) * P], identf)
                        z["peTR"].inc(i)
                    if ac:
                        z["peTR"].wait(e, T + 1)
                        z["acHT"].inc(e.activation(h0h[r][:, :], bank[0][:, 0:D], ACT.Copy))
                    if dv:
                        z["acHT"].wait(e, T + 1)
                        z["dvHT"].inc(e.tensor_tensor(h0l[r][:, :], bank[0][:, 0:D], h0h[r][:, :].bitcast(F32), ALU.subtract))

                def proj(o, th, tl, wh, wl, c0, n):
                    for k in range(KD):
                        lt, c = slice(k * P, (k + 1) * P), slice(c0, c0 + n)
                        i = three(o, th[:, lt], tl[:, lt], wh[:, k, c], wl[:, k, c], k == 0, k == KD - 1)
                    return i

                def qk(T, u):
                    r = u % 2
                    if pe:
                        z["dvHT"].wait(e, T + 1)
                        z["dvQK"].wait(e, T)
                        z["peQK"].inc(proj(bank[1][:, :], h0h[r], h0l[r], wa_h, wa_l, 0, 2 * D))
                    if dv:
                        z["peQK"].wait(e, T + 1)
                        z["acEX"].wait(e, T)
                        z["dvMN"].inc(e.tensor_scalar(mn[:, :], bank[1][:, :], 0.0, None, ALU.min))
                    if ac:
                        z["dvMN"].wait(e, T + 1)
                        z["dvQK"].wait(e, T)
                        z["acEX"].inc(e.activation(ex[:, :], mn[:, :], ACT.Exp))

                def feat(T, u):
                    r = u % 2
                    if dv:
                        z["acEX"].wait(e, T + 1)
                        z["peDL"].wait(e, T - 1)
                        z["peTQ"].wait(e, 2 * T - 2)
                        z["dvQK"].inc(e.scalar_tensor_tensor(
                            qkp[r][:, :, :, 0:D0].rearrange("p a h d -> p (a h) d"),
                            bank[1][:, :].rearrange("p (x d) -> p x d", d=D0), 0.0,
                            ex[:, :].rearrange("p (x d) -> p x d", d=D0), ALU.max, ALU.add))

                def v(T, u):
                    r = u % 2
                    if pe:
                        z["dvHT"].wait(e, T + 1)
                        z["dvX"].wait(e, T - 1)
                        z["peV"].inc(proj(bank[2][:, 0:D], h0h[r], h0l[r], wa_h, wa_l, 2 * D, D))
                    if ac:
                        z["peV"].wait(e, T + 1)
                        z["peNU"].wait(e, T - 1)
                        z["acV"].inc(e.activation(va[r][:, :, 0:D0], bank[2][:, 0:D].rearrange("p (h d) -> p h d", h=H0),
                                                  ACT.Copy))

                def tq(T, u, j):
                    r = u % 2
                    if pe:
                        z["dvQK"].wait(e, T + 1)
                        z["dvAT"].wait(e, 4 * (T - 1) + j + 1)
                        x = qkp[r][:, j, :, :].rearrange("p h d -> p (h d)")
                        for c in range(4):
                            i = e.transpose(bank[4 + j][:, c * P:(c + 1) * P], x[:, c * P:(c + 1) * P], identf)
                        z["peTQ"].inc(i)
                    if ac:
                        z["peTQ"].wait(e, 2 * T + j + 1)
                        z["acTQ"].inc(e.activation(flat((qT0, kT0)[j][r][:, :, :]), bank[4 + j][:, :], ACT.Copy))

                def sc(T, u, g_):
                    r = u % 2
                    if pe:
                        z["acTQ"].wait(e, 2 * T + 2)
                        z["dvAT"].wait(e, 4 * (T - 1) + g_ + 1)
                        rg = slice(32 * g_, 32 * g_ + 32)
                        for c in range(4):
                            i = e.matmul(bank[4 + g_][:, c * P:(c + 1) * P], kT0[r][rg, c, :], qT0[r][rg, c, :],
                                         start=True, stop=True)
                        z["peAT"].inc(i)
                    if dv:
                        z["peAT"].wait(e, 4 * T + g_ + 1)
                        z["peNU"].wait(e, T)
                        z["dvAT"].inc(e.tensor_tensor(
                            at[g_][:, :, :], bank[4 + g_][:, :].rearrange("p (c k) -> p c k", c=4),
                            causal.unsqueeze(1).to_broadcast([P, 4, P]), ALU.mult))

                def delta(T, u):
                    r = u % 2
                    if pe:
                        z["acV"].wait(e, T + 1)
                        z["dvQK"].wait(e, T + 1)
                        z["dvTY"].wait(e, T)
                        for c in range(4):
                            i = e.matmul(bank[0][:, c * 4 * VA:(c + 1) * 4 * VA],
                                         qkp[r][:, 1, 4 * c:4 * c + 4, :].rearrange("p h d -> p (h d)"),
                                         va[r][:, 4 * c:4 * c + 4, :].rearrange("p h d -> p (h d)"), start=True, stop=True)
                        z["peDL"].inc(i)
                    if dv:
                        z["peDL"].wait(e, T + 1)
                        z["dvSB"].wait(e, T)
                        keep = misc[:, bass.ds(T + MK, 1)]
                        z["dvDL"].inc(e.scalar_tensor_tensor(
                            dl[:, :, :], bank[0][:, 0:4 * 4 * VA].rearrange("p (c x) -> p c x", c=4), keep,
                            blk.unsqueeze(1).to_broadcast([P, 4, 4 * VA]), ALU.mult, ALU.mult))

                def num(T, u):
                    r = u % 2
                    if pe:
                        z["dvSB"].wait(e, T)
                        z["dvAT"].wait(e, 4 * T + 4)
                        z["acV"].wait(e, T + 1)
                        z["dvY"].wait(e, T)
                        for c in range(4):
                            e.matmul(bank[3][:, c * 4 * VA:(c + 1) * 4 * VA], qT0[r][:, c, :], Sbd[:, c, :],
                                     start=(c == 0), stop=False, skip_group_check=True)
                        for h in range(H0):
                            i = e.matmul(bank[3][:, h * VA:(h + 1) * VA], at[h % 4][:, h // 4, :], va[r][:, h, :],
                                         start=False, stop=(h == H0 - 1), skip_group_check=True)
                        z["peNU"].inc(i)
                    if dv:
                        z["peNU"].wait(e, T + 1)
                        z["dvDL"].wait(e, T + 1)
                        keep = misc[:, bass.ds(T + MK, 1)]
                        z["dvSB"].inc(e.scalar_tensor_tensor(flat(Sbd[:, :, :]), flat(Sbd[:, :, :]), keep, flat(dl[:, :, :]),
                                                             ALU.mult, ALU.add))
                        x = bank[3][:, 0:H0 * VA].rearrange("p (h d) -> p h d", h=H0)
                        z["dvDN"].inc(e.tensor_scalar(dn[:, :], x[:, :, D0], 1e-6, None, ALU.add))
                        z["dvDN"].wait(e, T + 1)
                        z["dvRC"].inc(e.reciprocal(rc[:, :], dn[:, :]))
                        z["dvRC"].wait(e, T + 1)
                        z["peTY"].wait(e, T)
                        z["dvY"].inc(e.tensor_tensor(y0[:, :].rearrange("p (h d) -> p h d", h=H0), x[:, :, 0:D0],
                                                     rc[:, :].unsqueeze(2).to_broadcast([P, H0, D0]), ALU.mult))

                def ty(T, u):
                    if pe:
                        z["dvY"].wait(e, T + 1)
                        z["dvHT"].wait(e, before(T + 2) + 1)
                        for k in range(KD):
                            i = e.transpose(bank[0][:, k * P:(k + 1) * P], y0[:, k * P:(k + 1) * P], identf)
                        z["peTY"].inc(i)
                    if ac:
                        z["peTY"].wait(e, T + 1)
                        z["pePR"].wait(e, T)
                        z["acTY"].inc(e.activation(yTh[:, :], bank[0][:, 0:D], ACT.Copy))
                    if dv:
                        z["acTY"].wait(e, T + 1)
                        z["dvTY"].inc(e.tensor_tensor(yTl[:, :], bank[0][:, 0:D], yTh[:, :].bitcast(F32), ALU.subtract))

                def pr(T, u):
                    if pe:
                        z["dvTY"].wait(e, T + 1)
                        z["acV"].wait(e, before(T + 1) + 1)
                        z["pePR"].inc(proj(bank[2][:, 0:D], yTh, yTl, wp_h, wp_l, 0, D))
                    if dv:
                        z["pePR"].wait(e, T + 1)
                        z["dvX"].inc(e.tensor_tensor(tile(X, T), bank[2][:, 0:D], tile(X, T), ALU.add))

                def y_stats(T, u):
                    r = u % 2
                    if dv:
                        z["dvX"].wait_alone(e, T + 1, s_passed)
                        z["dvYS"].inc(e.bn_stats(stats[1][:, r, :], tile(X, T)))
                        z["dvYS"].wait_alone(e, T + 1, s_passed)
                        z["dvYA"].inc(e.bn_aggr(meanvar[1][:, r, :], stats[1][:, r, :]))
                    if pl:
                        z["dvYA"].wait(e, T + 1)
                        z["plYR"].inc(e.tensor_tensor(rstd[1][:, r:r + 1], meanvar[1][:, r, 1:2], eps[:, 0:1], ALU.add))
                        z["plYR"].wait(e, 2 * T + 1)
                        z["plYR"].inc(e.tensor_tensor(rstd[1][:, r:r + 1], rstd[1][:, r:r + 1], mhalf[:, 0:1], ALU.pow))

                def y_norm(T, u):
                    r = u % 2
                    if dv:
                        z["plYR"].wait(e, 2 * T + 2)
                        z["dvYN"].inc(e.tensor_scalar(tile(Y, T), tile(X, T), meanvar[1][:, r, 0:1],
                                                      rstd[1][:, r:r + 1], ALU.subtract, ALU.mult))
                    if sp:
                        z["dvYN"].wait(e, T + 1)
                        row = P * T + (T // TB) + 1
                        s_ln["sST"].inc(e.dma_start(ya[bass.ds(row, P), :], tile(Y, T)[:, P:D]), 16)

                f = {"y_stats": y_stats, "y_norm": y_norm, "ln1": ln1, "ln2": ln2, "ht": ht, "qk": qk, "feat": feat, "v": v, "delta": delta, "num": num,
                     "ty": ty, "pr": pr, "qT": by(tq, 0), "kT": by(tq, 1)}
                for g_ in range(4):
                    f[f"sc{g_}"] = by(sc, g_)
                pipeline(LINEAR, f)
                z["dvYN"].wait(e, NT)
                if sp:
                    s_ln["sST"].wait(e, 16 * (GRP + NT))

            def loads_gate():
                def w(name):
                    return a[name].rearrange("(k p) n -> p k n", p=P)

                def row(name):
                    return a[name].rearrange("(a n) -> a n", a=1).to_broadcast([P, D])
                load(wkv[:, :, 0:D], w("L1_attn_Wk"), "raw")
                load(wkv[:, :, D:2 * D], w("L1_attn_Wv"), "raw")
                for dst, name in ((wqg, "L1_attn_Wq"), (wug, "L1_attn_Wu"), (wog, "L1_attn_Wo")):
                    load(dst, w(name), "raw")
                for dst, name in ((bkv[:, 0:D], "bk"), (bkv[:, D:2 * D], "bv"), (burow, "bu"), (lnw, "ln_w"), (lnb, "ln_b"),
                                  (borow, "bo")):
                    load(dst, row("L1_attn_" + name), "raw2")
                load(vec[:, 0:KD], a["L1_attn_bq"].rearrange("(k p) -> p k", p=P), "small", True)

            def gated_attention():
                if not sp:
                    loaded("raw")
                    loaded("raw2")
                    loaded("small")
                act(lambda: e.activation(wg_h[:, :], wgate, ACT.Copy))
                sync("dv", "A")
                dve(lambda: e.tensor_tensor(wg_l[:, :], wgate, wg_h[:, :].bitcast(F32), ALU.subtract))
                sync("pe", "V")
                bd = misc[:, MD:MD + P]
                NCL = 8

                def ln1(b):
                    if dv:
                        for t in range(TB):
                            i = e.bn_stats(st1[:, t, :], tile(X, TB * b + t))
                        g["dvST"].inc(i)
                        g["dvST"].wait_alone(e, b + 1, s_passed)
                        for t in range(TB):
                            i = e.bn_aggr(mv1[:, t, :], st1[:, t, :])
                        g["dvAG"].inc(i)
                    if pl:
                        g["dvAG"].wait(e, b + 1)
                        g["plRV"].inc(e.tensor_tensor(rv1[:, :], mv1[:, :, 1], eps[:, 0:TB], ALU.add))
                        g["plRV"].wait(e, 2 * b + 1)
                        g["plRV"].inc(e.tensor_tensor(rv1[:, :], rv1[:, :], mhalf[:, 0:TB], ALU.pow))

                def ln2(b, t):
                    T = TB * b + t
                    if dv:
                        g["plRV"].wait(e, 2 * b + 2)
                        g["peTR"].wait(e, T - 1)
                        g["dvXN"].inc(e.tensor_scalar(Xn1[t % 2][:, :], tile(X, T), mv1[:, t, 0:1], rv1[:, t:t + 1],
                                                      ALU.subtract, ALU.mult))

                def tr(b, t):
                    T = TB * b + t
                    if pe:
                        g["dvXN"].wait(e, T + 1)
                        g["dvHT"].wait(e, T)
                        g["dvTY"].wait(e, TB * b)
                        for k in range(KD):
                            i = e.transpose(bank[0][:, k * P:(k + 1) * P], Xn1[t % 2][:, k * P:(k + 1) * P], identf)
                        g["peTR"].inc(i)
                    if ac:
                        g["peTR"].wait(e, T + 1)
                        g["acHT"].inc(e.activation(h1h[:, :, t * P:(t + 1) * P],
                                                   bank[0][:, 0:D].rearrange("p (k x) -> p k x", k=KD), ACT.Copy))
                    if dv:
                        g["acHT"].wait(e, T + 1)
                        g["dvHT"].inc(e.tensor_tensor(h1l[:, :, t * P:(t + 1) * P],
                                                      bank[0][:, 0:D].rearrange("p (k x) -> p k x", k=KD),
                                                      h1h[:, :, t * P:(t + 1) * P].bitcast(F32), ALU.subtract))

                def of_tile(o, t, w):
                    for k in range(KD):
                        x = (slice(None), k, slice(t * P, (t + 1) * P))
                        i = three(o, h1h[x], h1l[x], w[0][:, k, :], w[1][:, k, :], k == 0, k == KD - 1)
                    return i

                def kv(b, t):
                    T = TB * b + t
                    o = bank[1 + t % 2]
                    if pe:
                        g["dvHT"].wait(e, T + 1)
                        g["dvKV"].wait(e, T - 1)
                        g["dvX"].wait(e, TB * b)
                        g["peKV"].inc(of_tile(o[:, :], t, wkv2))
                    if dv:
                        g["peKV"].wait(e, T + 1)
                        g["peKK"].wait(e, T - 1)
                        g["dvKV"].inc(e.tensor_tensor(kvb[t % 2][:, :], o[:, :], bkv, ALU.add))
                    if ac:
                        g["dvKV"].wait(e, T + 1)
                        g["peKK"].wait(e, T - 1)
                        g["acK"].inc(e.activation(kb[t % 2][:, :], kvb[t % 2][:, 0:D], ACT.Relu))

                def kk(b, t):
                    T = TB * b + t
                    if pe:
                        g["acK"].wait(e, T + 1)
                        if t == 0:
                            g["dvC"].wait(e, NCL * b)
                        for x in range(KD):
                            c = slice(x * P, (x + 1) * P)
                            i = e.matmul(bank[3][:, c], kb[t % 2][:, c], kvb[t % 2][:, D + x * P:D + (x + 1) * P],
                                         start=(t == 0 and x == 0), stop=(t == TB - 1 and x == KD - 1), skip_group_check=True)
                        g["peKK"].inc(i)

                def clamp(b):
                    if dv:
                        n = [NCL * b]
                        kv_ = bank[3][:, 0:D]

                        def do(i):
                            g["dvC"].inc(i)
                            n[0] = n[0] + 1
                            g["dvC"].wait(e, n[0])
                        g["peKK"].wait(e, TB * b + TB)
                        g["peO"].wait(e, TB * b)
                        do(e.tensor_scalar(ng[:, :], kv_, -1.0, None, ALU.mult))
                        do(e.tensor_tensor(ab[:, :], kv_, ng[:, :], ALU.max))
                        do(e.tensor_scalar(ab[:, :], ab[:, :], 0.01, 100.0, ALU.max, ALU.min))
                        do(e.tensor_scalar(sg[:, :], kv_, 0.0, None, ALU.is_gt))
                        do(e.tensor_scalar(ng[:, :], kv_, 0.0, None, ALU.is_lt))
                        do(e.tensor_tensor(sg[:, :], sg[:, :], ng[:, :], ALU.subtract))
                        do(e.tensor_tensor(ab[:, :], ab[:, :], sg[:, :], ALU.mult))
                        do(e.tensor_tensor(kvm[:, :].rearrange("p (a c) -> p a c", a=KD),
                                           ab[:, :].rearrange("p (a c) -> p a c", a=KD),
                                           bd.unsqueeze(1).to_broadcast([P, KD, P]), ALU.mult))

                def q(b):
                    for i in range(4):
                        c, hf = i // 2, i % 2
                        w = slice(hf * 512, (hf + 1) * 512)
                        o = bank[4 + i % 2]
                        if pe:
                            g["acQ"].wait(e, 4 * b + i - 1)
                            g["dvU"].wait(e, TB * b)
                            for k in range(KD):
                                wc = (slice(None), k, slice(c * P, (c + 1) * P))
                                ins = three(o[:, :], wqg2[0][wc], wqg2[1][wc], h1h[:, k, w], h1l[:, k, w], k == 0, k == KD - 1)
                            g["peQ"].inc(ins)
                        if ac:
                            g["peQ"].wait(e, 4 * b + i + 1)
                            g["acQ"].inc(e.activation(q1[:, c, w], o[:, :], ACT.Relu, bias=vec[:, c:c + 1]))

                def bo(b):
                    if pl:
                        g["dvXN"].wait(e, TB * b + TB)
                        v = X[:, bass.ds(TB * b, TB), :]
                        g["plBO"].inc(e.tensor_tensor(v, v, borow.unsqueeze(1).to_broadcast([P, TB, D]), ALU.add))

                def out_(b, t):
                    T = TB * b + t
                    o = bank[6 + t % 2][:, 0:D]
                    if pe:
                        g["acQ"].wait(e, 4 * b + 4)
                        g["dvC"].wait(e, NCL * b + NCL)
                        g["acO"].wait(e, T - 1)
                        for x in range(KD):
                            i = e.matmul(o[:, x * P:(x + 1) * P], q1[:, x, t * P:(t + 1) * P], kvm[:, x * P:(x + 1) * P],
                                         start=True, stop=True)
                        g["peO"].inc(i)
                    if dv:
                        g["peO"].wait(e, T + 1)
                        g["dvS2"].inc(e.bn_stats(st2[:, t, :], o))
                    if ac:
                        g["dvS2"].wait(e, T + 1)
                        g["dvO"].wait(e, TB * b)
                        g["acO"].inc(e.activation(oA[:, t, :], o, ACT.Copy))

                def ln3(b):
                    if dv:
                        g["dvS2"].wait_alone(e, TB * b + TB, s_passed)
                        for t in range(TB):
                            i = e.bn_aggr(mv2[:, t, :], st2[:, t, :])
                        g["dvA2"].inc(i)
                    if pl:
                        g["dvA2"].wait(e, b + 1)
                        g["plR2"].inc(e.tensor_tensor(rv2[:, :], mv2[:, :, 1], eps[:, 0:TB], ALU.add))
                        g["plR2"].wait(e, 2 * b + 1)
                        g["plR2"].inc(e.tensor_tensor(rv2[:, :], rv2[:, :], mhalf[:, 0:TB], ALU.pow))

                def u_(b, t):
                    T = TB * b + t
                    r = t % 2
                    o = bank[4 + r][:, 0:D]
                    if pe:
                        g["dvU"].wait(e, T - 1)
                        g["acQ"].wait(e, 4 * b + 4)
                        g["peU"].inc(of_tile(o, t, wug2))
                    if dv:
                        g["plR2"].wait(e, 2 * b + 2)
                        g["acO"].wait(e, TB * b + t + 1)
                        g["dvY"].wait(e, T - 1)
                        g["dvO"].inc(e.tensor_scalar(o1[r][:, :], oA[:, t, :], mv2[:, t, 0:1], rv2[:, t:t + 1],
                                                     ALU.subtract, ALU.mult))
                        g["peU"].wait(e, T + 1)
                        g["dvU"].inc(e.tensor_tensor(us[r][:, :], o, burow, ALU.add))
                    if pl:
                        g["dvO"].wait(e, T + 1)
                        g["plO"].inc(e.tensor_tensor(o1[r][:, :], o1[r][:, :], lnw, ALU.mult))
                        g["plO"].wait(e, 2 * T + 1)
                        g["plO"].inc(e.tensor_tensor(o1[r][:, :], o1[r][:, :], lnb, ALU.add))

                def y_(b, t):
                    T = TB * b + t
                    r = t % 2
                    if dv:
                        g["plO"].wait(e, 2 * T + 2)
                        g["dvU"].wait(e, T + 1)
                        g["peTY"].wait(e, T - 1)
                        g["dvY"].inc(e.tensor_tensor(y1[r][:, :], us[r][:, :], o1[r][:, :], ALU.mult))
                    if pe:
                        g["dvY"].wait(e, T + 1)
                        g["dvHT"].wait(e, TB * b + TB)
                        g["dvTY"].wait(e, T)
                        for k in range(KD):
                            i = e.transpose(bank[0][:, k * P:(k + 1) * P], y1[r][:, k * P:(k + 1) * P], identf)
                        g["peTY"].inc(i)
                    if ac:
                        g["peTY"].wait(e, T + 1)
                        g["pePR"].wait(e, T - 1)
                        g["acTY"].inc(e.activation(y1h[r][:, :], bank[0][:, 0:D], ACT.Copy))

                def y_low(b, t):
                    T = TB * b + t
                    r = t % 2
                    if dv:
                        g["acTY"].wait(e, T + 1)
                        g["dvTY"].inc(e.tensor_tensor(y1l[r][:, :], bank[0][:, 0:D], y1h[r][:, :].bitcast(F32), ALU.subtract))

                def pr(b, t):
                    T = TB * b + t
                    r = t % 2
                    o = bank[1 + r][:, 0:D]
                    if pe:
                        g["dvTY"].wait(e, T + 1)
                        g["dvKV"].wait(e, TB * b + TB)
                        g["dvX"].wait(e, T - 1)
                        for k in range(KD):
                            lt = slice(k * P, (k + 1) * P)
                            i = three(o, y1h[r][:, lt], y1l[r][:, lt], wog2[0][:, k, :], wog2[1][:, k, :], k == 0, k == KD - 1)
                        g["pePR"].inc(i)
                    if dv:
                        g["pePR"].wait(e, T + 1)
                        g["plBO"].wait(e, b + 1)
                        g["dvX"].inc(e.tensor_tensor(tile(X, T), o, tile(X, T), ALU.add))

                def batch(b, last):
                    ln2(b, 0)
                    ln2(b, 1)
                    tr(b, 0)
                    for t in range(TB):
                        if t + 2 < TB:
                            ln2(b, t + 2)
                        if t + 1 < TB:
                            tr(b, t + 1)
                        kv(b, t)
                        if t > 0:
                            kk(b, t - 1)
                    kk(b, TB - 1)
                    bo(b)
                    clamp(b)
                    q(b)
                    if not last:
                        ln1(b + 1)
                    for t in range(TB):
                        out_(b, t)
                    ln3(b)
                    for t in range(TB + 3):
                        if 1 <= t <= TB:
                            y_(b, t - 1)
                        if dv and t >= 3:
                            pr(b, t - 3)
                        if t < TB:
                            u_(b, t)
                        if 1 <= t <= TB:
                            y_low(b, t - 1)
                        if not dv and 2 <= t < TB + 2:
                            pr(b, t - 2)

                ln1(0)
                loop(B - 1, lambda b: batch(b, False))
                batch(B - 1, True)
                g["dvX"].wait(e, NT)

            loads_A(0)
            if sp:
                for n in range(GRP):
                    if n >= 2:
                        s_x[n % 2].wait(e, 16 * (n // 2))
                    s_x[n % 2].inc(e.dma_start(X[:, U * n:U * n + U, :], x_v[:, U * n:U * n + U, :]), 16)
            for c in range(2):
                for l in range(DEPTH):
                    run = DEPTH * c + l
                    if run == 0:
                        prep_A()
                        ln_pass()
                        first_tiles(run)
                    else:
                        first_tiles(run)
                        prep_A()
                    loads_B(l)
                    pass_A(run)
                    following = (lambda: loads_A(l + 1)) if l + 1 < DEPTH else loads_lin if c == 0 else loads_F
                    ffn(run, CH * GRP * run, True, next_loads=following)
                if c == 0:
                    linear_attention()
            merge()
            prep_F()
            loads_gate()
            ffn(NRUN, CH * GRP * NRUN, False)
            gated_attention()
            ffn(NRUN + 1, CH * GRP * NRUN + CF * GRP, False, True)

        @block.tensor
        def _(e):
            program("pe", e)

        @block.scalar
        def _(e):
            program("ac", e)

        @block.vector
        def _(e):
            program("dv", e)

        @block.gpsimd
        def _(e):
            program("pl", e)

        @block.sync
        def _(e):
            program("sp", e)


def kernel(**inputs):
    import numpy as _np
    import concourse.bacc as _bacc
    from concourse import mybir as _mybir
    from concourse.bass_utils import run_bass_kernel_spmd as _run

    nc = _bacc.Bacc("TRN2", target_bir_lowering=False, num_devices=1)
    arrays, args = {}, {}
    for name, v in {**inputs, **shape_constants()}.items():
        v = _np.ascontiguousarray(v)
        arrays[f"in_{name}"] = v
        args[name] = nc.dram_tensor(f"in_{name}", v.shape, _mybir.dt.from_np(v.dtype), kind="ExternalInput").ap()
    out = nc.dram_tensor("out_0", (B, N, D), F32, kind="ExternalOutput").ap()
    build(nc, args, out)
    r = _run(nc, [arrays], core_ids=[0])
    return r.results[0]["out_0"]
```
